# Optimizing a Trainium2 kernel written in Bass

```python
import numpy as np
import jax
import jax.numpy as jnp

def _softmax(x, axis=-1):
    return jax.nn.softmax(x, axis=axis)

def _gelu(x):
    return jax.nn.gelu(x, approximate=True)

def _silu(x):
    return jax.nn.silu(x)

def _sigmoid(x):
    return jax.nn.sigmoid(x)

def _layernorm(x, axis=-1, eps=1e-05):
    m = jnp.mean(x, axis=axis, keepdims=True)
    v = jnp.var(x, axis=axis, keepdims=True)
    return (x - m) / jnp.sqrt(v + eps)

def _scatter_add(tgt, idx, src, axis=0):
    return tgt.at[idx].add(src)

def _segment_sum(src, seg, n):
    return jax.ops.segment_sum(src, seg, n)
kernel_name = 'mk_conv_attn_hybrid_d2_conv_nchw256_r4_55dfe7'

def setup_inputs(seed: int=0):
    np.random.seed(seed)
    _w = jnp.asarray

    def _rec_inputs():
        import jax
        import jax.numpy as jnp
        _gk = jax.random.key(seed)
        x = -0.0002091 + 1 * jax.random.normal(jax.random.fold_in(_gk, 1), (32, 64, 56, 56), jnp.float32)
        return x
    x = _rec_inputs()

    def _L0_conv_setup():
        import jax, jax.numpy as jnp
        import numpy as np
        key = jax.random.key(seed)
        k1, k2 = jax.random.split(key)
        x = jax.random.normal(k1, (32, 64, 56, 56), dtype=jnp.float32)
        fan_in = 64 * 3 * 3
        bound = 1.0 / np.sqrt(fan_in)
        weight = jax.random.uniform(k2, (64, 64, 3, 3), dtype=jnp.float32, minval=-bound, maxval=bound)
        return {'x': x, 'weight': weight}
    _L0_conv_all = _L0_conv_setup()
    _L0_conv_in = {k: v for k, v in _L0_conv_all.items() if k in ('weight',)}
    del _L0_conv_all

    def _L1_attn_setup():
        import jax, jax.numpy as jnp
        import numpy as np
        B, S, D, U = (8, 512, 64, 32)
        key = jax.random.key(seed)
        ks = jax.random.split(key, 5)
        inputs = jax.random.normal(ks[0], (B, S, D), dtype=jnp.float32)
        W_q = jax.random.normal(ks[1], (D, U), dtype=jnp.float32) * (1.0 / np.sqrt(D))
        W_k = jax.random.normal(ks[2], (D, U), dtype=jnp.float32) * (1.0 / np.sqrt(D))
        W_v = jax.random.normal(ks[3], (D, U), dtype=jnp.float32) * (1.0 / np.sqrt(D))
        W_o = jax.random.normal(ks[4], (U, D), dtype=jnp.float32) * (1.0 / np.sqrt(U))
        b_o = jnp.zeros((D,), dtype=jnp.float32)
        return {'inputs': inputs, 'W_q': W_q, 'W_k': W_k, 'W_v': W_v, 'W_o': W_o, 'b_o': b_o}
    _L1_attn_all = _L1_attn_setup()
    _L1_attn_in = {k: v for k, v in _L1_attn_all.items() if k in ('W_q', 'W_k', 'W_v', 'W_o', 'b_o')}
    del _L1_attn_all

    def _L1_ffn_setup():
        import jax, jax.numpy as jnp
        import numpy as np
        BN_EPS = 0.001

        def _bn(h, g, b, m, v):
            return g * (h - m) * jax.lax.rsqrt(v + BN_EPS) + b
        key = jax.random.key(seed)
        ks = jax.random.split(key, 8)
        B, F, Df = (64, 16, 64)
        E, H, D = (8, 64, 64)
        s1 = 1.0 / np.sqrt(Df)
        s2 = 1.0 / np.sqrt(H)
        return {'x': jax.random.normal(ks[0], (B, F, Df), jnp.float32), 'Wr': jax.random.normal(ks[1], (Df, E), jnp.float32) * s1, 'br': jnp.zeros((E,), jnp.float32), 'W1': jax.random.normal(ks[2], (E, Df, H), jnp.float32) * s1, 'b1': jnp.zeros((E, H), jnp.float32), 'g1': jnp.ones((E, H), jnp.float32), 'be1': jnp.zeros((E, H), jnp.float32), 'm1': jnp.zeros((E, H), jnp.float32), 'v1': jnp.ones((E, H), jnp.float32), 'W2': jax.random.normal(ks[3], (E, H, H), jnp.float32) * s2, 'b2': jnp.zeros((E, H), jnp.float32), 'g2': jnp.ones((E, H), jnp.float32), 'be2': jnp.zeros((E, H), jnp.float32), 'm2': jnp.zeros((E, H), jnp.float32), 'v2': jnp.ones((E, H), jnp.float32), 'Wo': jax.random.normal(ks[4], (E, H, D), jnp.float32) * s2, 'bo': jnp.zeros((E, D), jnp.float32)}
    _L1_ffn_all = _L1_ffn_setup()
    _L1_ffn_in = {k: v for k, v in _L1_ffn_all.items() if k in ('Wr', 'br', 'W1', 'b1', 'g1', 'be1', 'm1', 'v1', 'W2', 'b2', 'g2', 'be2', 'm2', 'v2', 'Wo', 'bo')}
    del _L1_ffn_all
    return {'x': x, 'L0_conv_weight': _L0_conv_in['weight'], 'L1_attn_W_q': _L1_attn_in['W_q'], 'L1_attn_W_k': _L1_attn_in['W_k'], 'L1_attn_W_v': _L1_attn_in['W_v'], 'L1_attn_W_o': _L1_attn_in['W_o'], 'L1_attn_b_o': _L1_attn_in['b_o'], 'L1_ffn_Wr': _L1_ffn_in['Wr'], 'L1_ffn_br': _L1_ffn_in['br'], 'L1_ffn_W1': _L1_ffn_in['W1'], 'L1_ffn_b1': _L1_ffn_in['b1'], 'L1_ffn_g1': _L1_ffn_in['g1'], 'L1_ffn_be1': _L1_ffn_in['be1'], 'L1_ffn_m1': _L1_ffn_in['m1'], 'L1_ffn_v1': _L1_ffn_in['v1'], 'L1_ffn_W2': _L1_ffn_in['W2'], 'L1_ffn_b2': _L1_ffn_in['b2'], 'L1_ffn_g2': _L1_ffn_in['g2'], 'L1_ffn_be2': _L1_ffn_in['be2'], 'L1_ffn_m2': _L1_ffn_in['m2'], 'L1_ffn_v2': _L1_ffn_in['v2'], 'L1_ffn_Wo': _L1_ffn_in['Wo'], 'L1_ffn_bo': _L1_ffn_in['bo']}

def reference(x, L0_conv_weight, L1_attn_W_q, L1_attn_W_k, L1_attn_W_v, L1_attn_W_o, L1_attn_b_o, L1_ffn_Wr, L1_ffn_br, L1_ffn_W1, L1_ffn_b1, L1_ffn_g1, L1_ffn_be1, L1_ffn_m1, L1_ffn_v1, L1_ffn_W2, L1_ffn_b2, L1_ffn_g2, L1_ffn_be2, L1_ffn_m2, L1_ffn_v2, L1_ffn_Wo, L1_ffn_bo):
    import jax
    import jax.numpy as jnp

    def _L0_conv_ref(x, weight):
        import jax, jax.numpy as jnp
        import numpy as np
        bw = jnp.sign(weight)
        out = jax.lax.conv_general_dilated(x, bw, window_strides=(1, 1), padding=((1, 1), (1, 1)), dimension_numbers=('NCHW', 'OIHW', 'NCHW'))
        return out

    def _L1_attn_ref(inputs, W_q, W_k, W_v, W_o, b_o):
        import jax, jax.numpy as jnp
        import numpy as np
        B, S, D, U = (8, 512, 64, 32)
        Q = jnp.einsum('bsd,du->bsu', inputs, W_q)
        K = jnp.einsum('bsd,du->bsu', inputs, W_k)
        V = jnp.einsum('bsd,du->bsu', inputs, W_v)
        scale = 1.0 / jnp.sqrt(jnp.asarray(U, dtype=inputs.dtype))
        attn = jnp.einsum('bqu,bku->bqk', Q, K) * scale
        w = jax.nn.softmax(attn, axis=-1)
        out = jnp.einsum('bqk,bku->bqu', w, V)
        return jnp.einsum('bsu,ud->bsd', out, W_o) + b_o + inputs

    def _L1_ffn_ref(x, Wr, br, W1, b1, g1, be1, m1, v1, W2, b2, g2, be2, m2, v2, Wo, bo):
        import jax, jax.numpy as jnp
        import numpy as np
        BN_EPS = 0.001

        def _bn(h, g, b, m, v):
            return g * (h - m) * jax.lax.rsqrt(v + BN_EPS) + b
        feat = jnp.mean(x, axis=0)
        w = jax.nn.softmax(feat @ Wr + br, axis=-1)
        h = jnp.einsum('bfd,edh->bfeh', x, W1) + b1
        h = jax.nn.relu(_bn(h, g1, be1, m1, v1))
        h = jnp.einsum('bfeh,ehk->bfek', h, W2) + b2
        h = jax.nn.relu(_bn(h, g2, be2, m2, v2))
        y = jnp.einsum('bfeh,ehd->bfed', h, Wo) + bo
        return jnp.einsum('bfed,fe->bfd', y, w)

    def _gn(v, G=32, eps=1e-05):
        B_, C_, H_, W_ = v.shape
        g = v.reshape(B_, G, C_ // G, H_, W_)
        m = jnp.mean(g, axis=(2, 3, 4), keepdims=True)
        s = jnp.var(g, axis=(2, 3, 4), keepdims=True)
        return ((g - m) / jnp.sqrt(s + eps)).reshape(v.shape)

    def _ln_c(v, eps=1e-06):
        m = jnp.mean(v, axis=1, keepdims=True)
        s = jnp.var(v, axis=1, keepdims=True)
        return (v - m) / jnp.sqrt(s + eps)

    def _ln_t(v, eps=1e-05):
        m = jnp.mean(v, axis=-1, keepdims=True)
        s = jnp.var(v, axis=-1, keepdims=True)
        return (v - m) / jnp.sqrt(s + eps)

    def _to_tokens(v):
        B_, C_, H_, W_ = v.shape
        return v.reshape(B_, C_, H_ * W_).transpose(0, 2, 1)

    def _from_tokens(t, like):
        B_, C_, H_, W_ = like.shape
        return t.transpose(0, 2, 1).reshape(B_, C_, H_, W_)
    x = x + _L0_conv_ref(_gn(x), L0_conv_weight)
    t = _to_tokens(x)
    t = t + _L1_attn_ref(_ln_t(t), L1_attn_W_q, L1_attn_W_k, L1_attn_W_v, L1_attn_W_o, L1_attn_b_o)
    t = t + _L1_ffn_ref(_ln_t(t), L1_ffn_Wr, L1_ffn_br, L1_ffn_W1, L1_ffn_b1, L1_ffn_g1, L1_ffn_be1, L1_ffn_m1, L1_ffn_v1, L1_ffn_W2, L1_ffn_b2, L1_ffn_g2, L1_ffn_be2, L1_ffn_m2, L1_ffn_v2, L1_ffn_Wo, L1_ffn_bo)
    x = _from_tokens(t, x)
    return x

_drawn_inputs = setup_inputs


def setup_inputs(seed=0):
    import zlib

    import numpy as np

    out = dict(_drawn_inputs(seed))
    spreads = {'L1_attn_b_o': (0.0, 0.8),
     'L1_ffn_br': (0.0, 0.8),
     'L1_ffn_b1': (0.0, 0.8),
     'L1_ffn_g1': (1.0, 0.6),
     'L1_ffn_be1': (0.0, 0.8),
     'L1_ffn_m1': (0.0, 0.8),
     'L1_ffn_v1': (1.0, 0.6),
     'L1_ffn_b2': (0.0, 2.0),
     'L1_ffn_g2': (1.0, 0.6),
     'L1_ffn_be2': (0.0, 2.0),
     'L1_ffn_m2': (0.0, 2.0),
     'L1_ffn_v2': (1.0, 0.6),
     'L1_ffn_bo': (0.0, 2.0)}
    factors = {'L1_attn_W_q': 8.0,
     'L1_attn_W_k': 8.0,
     'L1_attn_W_v': 8.0,
     'L1_attn_W_o': 8.0,
     'L1_ffn_Wr': 8.0,
     'L1_ffn_W1': 8.0,
     'L1_ffn_W2': 8.0,
     'L1_ffn_Wo': 7.396}
    for name, (base, spread) in spreads.items():
        noise = np.random.default_rng([zlib.crc32(name.encode()), seed]).standard_normal(out[name].shape)
        drawn = base * np.exp(spread * noise) if base else spread * noise
        out[name] = jnp.asarray(drawn.astype(out[name].dtype))
    for name, factor in factors.items():
        out[name] = (out[name] * factor).astype(out[name].dtype)
    return out
```

```python
import numpy as np
import concourse.bass as bass
from concourse import mybir
from contextlib import ExitStack

F32, F32R = mybir.dt.float32, mybir.dt.float32r
ALU, ACT, AX = mybir.AluOpType, mybir.ActivationFunctionType, mybir.AxisListType

P = 128
C = 64
HW = 56
PAIRS = HW // 2
HALF = PAIRS * HW
S = 2 * HALF
U = 32
HID, EXP = 64, 8
EP = EXP // 2
CH = 4
CW = HALF // CH
CP = PAIRS // CH
QC = 8
QW = HALF // QC
KB = -(-S // P)
SP = KB * P
MC = 7
MW = S // MC
KS = 3 * U
MR = 4
NMR = -(-KB // MR)
AHEAD = 4
PADW = HW + 2
RB = -(-HALF // P)
RW = RB * P
SCALE = 1.0 / float(np.sqrt(U))

N_M0 = 4 * CH + AHEAD * MR * MC + AHEAD
N_M = 4 * CH + KB * MC + NMR
STEPS = KB + 1
SLOT = QC * STEPS


def timeline(lag):
    order = []
    for c in range(QC):
        for k in range(0, KB, 2):
            order.append((c * STEPS + k, "attend", "score", (c, k)))
            if k + 1 < KB:
                order.append((c * STEPS + k + 1, "attend", "score", (c, k + 1)))
            order.append((c * STEPS + k + 3.1, "attend", "value", (c, k)))
        order.append(((c + 1) * STEPS + 4 + lag, "attend", "project", (c,)))
        order.append(((c + 1) * STEPS + 1.5, "attend", "gather", (c,)))
    at = 1
    for kind, q in (("mean", 0), ("mean", 1), ("var", 0), ("mean", 2), ("var", 1), ("mean", 3), ("var", 2), ("var", 3)):
        order.append((at + lag, "norms", kind, (q,)))
        if kind == "var":
            order.append((at + 5 + lag, "norms", "hi", (q,)))
        at += 3
    order += [(0, "prepare", "stats", ()), (9 + lag, "prepare", "pair", ()), (12 + lag, "prepare", "shift", ())]
    order += [(14 + 2 * r + lag, "prepare", "pad", (r,)) for r in range(CH)]
    at = 28
    for kind, q in (("conv", 0), ("mean", 0), ("conv", 1), ("var", 0), ("mean", 1), ("conv", 2), ("var", 1), ("mean", 2),
                    ("conv", 3), ("var", 2), ("mean", 3), ("var", 3)):
        order.append((at + lag, "prepare", kind, (q,)))
        if kind == "var":
            order += [(at + 7 + 2 * n, "prepare", "proj", (q, n)) for n in range(4)]
        at += 3
    order += [(at + 7 + 3 * n + lag, "prepare", "values", (n,)) for n in range(2)]
    border = at + 20
    ahead = AHEAD * MR
    for b in range(KB):
        start, blocks, places, stage = (border, ahead, SLOT - 2 - border, "prepare") if b < ahead else (0.5, KB - ahead, border - 2, "attend")
        for m in range(MC):
            place = start + (b % ahead * MC + m) * places / (blocks * MC)
            order.append((place, stage, "max", (b, m)))
        if b % MR == MR - 1 or b == KB - 1:
            order.append((place + 0.01, stage, "blockmax", (b // MR,)))
            order.append((place + 1.4, stage, "row", (b // MR,)))
    return sorted(order, key=lambda entry: entry[0])


def rows_needed(c):
    return -(-(c + 1) * 2 * QW // (P * MR))


class Place:

    def __init__(self, slot, use, after):
        self.slot, self.use, self.after = slot, use, after

    def m(self, n):
        return n if self.slot is None else self.slot.count(N_M, N_M0 + n)

    def bank(self):
        return (self.use + (0 if self.slot is None else self.slot.c * N_M + N_M0)) % 2


class Image:

    def __init__(self, c, t=None):
        self.c, self.t, self.parity = c, t, c % 2

    def count(self, per, n):
        return self.c * per + n if self.t is None else self.t * (2 * per) + (self.c * per + n)

    def number(self):
        return self.c if self.t is None else self.t * 2 + self.c


def wait(engine, semaphore, value):
    if not isinstance(value, int) or value > 0:
        engine.wait_ge(semaphore, value)


def wait_apart(engine, semaphore, value, passed):
    wait(engine, semaphore, value)
    engine.sem_inc(passed, 1)


def walk(engine, images, lag, step):
    order = timeline(lag)

    def slot(prepare, attend, norms):
        stages = {"prepare": prepare, "attend": attend, "norms": norms}
        uses, after = {}, {}
        for _, stage, kind, args in order:
            if stages[stage] is not None:
                if kind in ("proj", "max", "row"):
                    uses[kind, args] = len(uses)
                elif kind == "blockmax":
                    after[kind, args] = uses["max", (min(args[0] * MR + MR, KB) - 1, MC - 1)] + 1
                elif kind == "score" and args[1] == 0:
                    needed = rows_needed(args[0]) - 1
                    after[kind, args] = 0 if needed < AHEAD else uses["row", (needed,)] + 1
        at = attend if attend is not None else norms
        for _, stage, kind, args in order:
            if stages[stage] is not None:
                place = Place(None if attend is None and norms is None else at, uses.get((kind, args)), after.get((kind, args)))
                step(stage, kind, stages[stage], place, *args)

    slot(Image(0), None, None)
    slot(Image(1), Image(0), None)
    loops = (images - 2) // 2
    with engine.Fori(0, loops) as t:
        for j in range(2):
            slot(Image(j + 2, t), Image(j + 1, t), Image(j, t))
    slot(None, Image(images - 1), Image(images - 2))
    slot(None, None, Image(images - 1))


def attention_phase(nc, images, x, conv_w, w_q, w_k, w_v, w_o, b_o, ident_in, block_in, pair_in, t2_dram, hi_dram, lo_dram, ident, feat):
    x_rows = x.rearrange("i c (r a) w -> i a c r w", a=2)
    x_flat = x.rearrange("i c h w -> i c (h w)")

    ctx = ExitStack()
    with ctx:
        def sb(name, shape, dt=F32):
            return ctx.enter_context(nc.sbuf_tensor(name, shape, dt))

        def sem(name):
            return ctx.enter_context(nc.semaphore(name))

        block, pair = sb("block", [P, P]), sb("pair", [P, P])
        ident_r = sb("ident_r", [P, P], F32R)
        eps5 = sb("eps5", [P, 1])
        conv_raw = sb("conv_raw", [C, C, 9])
        conv_neg = sb("conv_neg", [C, C, 9])
        conv_sign = sb("conv_sign", [C, 9, 2, C])
        conv_st = sb("conv_st", [P, 4, 3, P], F32R)
        wq_st, wk_st = sb("wq_st", [P, 4, U]), sb("wk_st", [P, 4, U])
        wv_st = sb("wv_st", [P, U])
        wo_st, den_st = sb("wo_st", [P, C]), sb("den_st", [P, C])
        bo_col = sb("bo_col", [P, 1])
        xin = sb("xin", [P, S])
        xpk = sb("xpk", [P, HALF])
        pad = sb("pad", [P, HW + 2, PADW], F32R)
        stats, mv, mv2 = sb("stats", [P, MC, 6]), sb("mv", [P, 2]), sb("mv2", [P, 2])
        gm, gsq, gvar, gln, gs, gb = (sb(n, [P, 2]) for n in ("gm", "gsq", "gvar", "gln", "gs", "gb"))
        tres, xn = sb("tres", [P, HALF]), sb("xn", [P, HALF])
        sq, rstd = sb("sq", [P, 2, CW]), sb("rstd", [P, 2, CW])
        base = sb("base", [P, 2, HALF])
        qs = [sb(f"qs{j}", [P, SP], F32R) for j in range(2)]
        ks = [sb(f"ks{j}", [P, SP], F32R) for j in range(2)]
        vs = [sb(f"vs{j}", [P, KB, C]) for j in range(2)]
        part_max, block_max = sb("part_max", [P, KB, MC]), sb("block_max", [P, NMR * MR])
        neg_max = sb("neg_max", [P, KS + NMR * MR], F32R)
        probs = sb("probs", [P, 4, 2 * QW])
        osb = sb("osb", [P, 2, 2 * QW])
        rden, onorm = sb("rden", [P, QW]), sb("onorm", [P, QW])
        t2 = sb("t2", [P, 2, HALF])
        xn2 = sb("xn2", [P, HALF])
        sq2, rstd2 = sb("sq2", [P, 2, CW]), sb("rstd2", [P, 2, CW])
        hi, lo = sb("hi", [P, HALF], F32R), sb("lo", [P, HALF], F32R)

        pb = [ctx.enter_context(nc.psum_tensor(f"bank{j}", [P, 512], F32)) for j in range(8)]
        s_bank, o_bank, m_bank, x0, x1 = pb[0:3], pb[3], pb[4:6], pb[6], pb[7]

        conv_loaded, loaded_w, weights_ready, setup = sem("conv_loaded"), sem("loaded_w"), sem("weights_ready"), sem("setup")
        signs_ready, conv_turned, fills_done = sem("signs_ready"), sem("conv_turned"), sem("fills_done")
        x_loaded, xpk_loaded = sem("x_loaded"), sem("xpk_loaded")
        dve_chain, pool_chain, dve_passed, pool_passed = sem("dve_chain"), sem("pool_chain"), sem("dve_passed"), sem("pool_passed")
        moments_ready, pair_done, gvar_ready, gln_ready, gs_ready, gb_ready = (
            sem(n) for n in ("moments_ready", "pair_done", "gvar_ready", "gln_ready", "gs_ready", "gb_ready"))
        pad_hi, pad_lo = sem("pad_hi"), sem("pad_lo")
        conv_done, tres_ready, mean_done, cent_ready, sq_ready, var_done, rln_ready, rstd_ready, xn_ready, base_ready = (
            sem(n) for n in ("conv_done", "tres_ready", "mean_done", "cent_ready", "sq_ready", "var_done", "rln_ready", "rstd_ready", "xn_ready", "base_ready"))
        m_done, part_hi, m_used = sem("m_done"), sem("part_hi"), sem("m_used")
        v_done, v_ready = sem("v_done"), sem("v_ready")
        negmax_ready, row_done, row_ready = sem("negmax_ready"), sem("row_done"), sem("row_ready")
        s_done, p_ready, o_done, o_saved, proj_done, t2_ready = (sem(n) for n in ("s_done", "p_ready", "o_done", "o_saved", "proj_done", "t2_ready"))
        mean2_done, cent2_ready, sq2_ready, var2_done, rln2_ready, rstd2_ready, xn2_ready, feat_ready, hi_ready, lo_ready = (
            sem(n) for n in ("mean2_done", "cent2_ready", "sq2_ready", "var2_done", "rln2_ready", "rstd2_ready", "xn2_ready", "feat_ready", "hi_ready", "lo_ready"))
        t2_stored, hi_stored, lo_stored = sem("t2_stored"), sem("hi_stored"), sem("lo_stored")

        def proj_cols(tile, part, q, n):
            if n < 2:
                return tile[part, 0:S].rearrange("p (c a i) -> p c a i", a=2, i=QW)[:, q * CW // QW:(q + 1) * CW // QW, n, :]
            return tile[part, (n - 2) * HALF + q * CW:(n - 2) * HALF + (q + 1) * CW]

        def piece(tile, q):
            return tile[:, q * CW:(q + 1) * CW]

        with nc.Block() as block1:
            @block1.sync
            def _(sp):
                def load(dst, src):
                    sp.dma_start(dst, src).then_inc(loaded_w, 16)
                sp.dma_start(conv_raw[:], conv_w.rearrange("o i a b -> o i (a b)")).then_inc(conv_loaded, 16)
                load(ident[:], ident_in)
                load(block[:], block_in)
                load(pair[:], pair_in)
                for h in range(2):
                    rows = slice(h * C, (h + 1) * C)
                    for r in range(4):
                        load(wq_st[rows, r, :], w_q)
                        load(wk_st[rows, r, :], w_k)
                    load(wv_st[rows, :], w_v)
                    load(bo_col[rows, :], b_o.rearrange("(c a) -> c a", a=1))
                sp.wait_ge(fills_done, 1)
                load(wo_st[0:U, :], w_o)
                load(wo_st[C:C + U, :], w_o)

                def fetch(image):
                    n = image.number()
                    if image.c or image.t is not None:
                        sp.wait_ge(pad_hi, image.count(CH, 0))
                        sp.wait_ge(pad_lo, image.count(CH, 0))
                        sp.wait_ge(tres_ready, image.count(CH, 0))
                    src = x_flat[bass.ds(n, 1)].rearrange("i c n -> (i c) n")
                    for h in range(2):
                        sp.dma_start(xin[h * C:(h + 1) * C, :], src).then_inc(x_loaded, 16)
                    for h in range(2):
                        sp.dma_start(xpk[h * C:(h + 1) * C, :].rearrange("c (r w) -> c r w", w=HW),
                                     x_rows[bass.ds(n, 1), h].rearrange("i c r w -> (i c) r w")).then_inc(xpk_loaded, 16)

                def store(image):
                    n, par = image.number(), image.parity

                    def to(dram):
                        return dram[bass.ds(n, 1)].rearrange("i a c n -> (i a c) n")
                    sp.wait_ge(t2_ready, image.count(3 * QC, 3 * QC))
                    sp.dma_start(to(t2_dram), t2[:, par, :]).then_inc(t2_stored, 16)
                    sp.wait_ge(hi_ready, image.count(CH, CH))
                    sp.dma_start(to(hi_dram), hi[:].bitcast(F32)).then_inc(hi_stored, 16)
                    sp.wait_ge(lo_ready, image.count(CH, CH))
                    sp.dma_start(to(lo_dram), lo[:].bitcast(F32)).then_inc(lo_stored, 16)

                fetch(Image(0))
                fetch(Image(1))
                fetch(Image(2))
                store(Image(0))
                fetch(Image(3))
                store(Image(1))
                loops = (images - 4) // 2
                with sp.Fori(0, loops) as t:
                    for j in range(2):
                        fetch(Image(4 + j, t))
                        store(Image(2 + j, t))
                store(Image(images - 2))
                store(Image(images - 1))
                sp.wait_ge(t2_stored, 16 * images)
                sp.wait_ge(hi_stored, 16 * images)
                sp.wait_ge(lo_stored, 16 * images)

            @block1.gpsimd
            def _(gp):
                gp.memset(wo_st[:], 0.0).then_inc(fills_done, 1)
                gp.memset(den_st[:], 0.0)
                gp.memset(pad[:].bitcast(F32), 0.0)
                gp.memset(conv_st[:].bitcast(F32), 0.0)
                gp.memset(eps5[:], 1e-5)
                gp.memset(neg_max[:].bitcast(F32), 0.0)
                gp.memset(feat[:], 0.0)
                gp.memset(probs[:], 0.0)
                for j in range(2):
                    gp.memset(qs[j][:].bitcast(F32), 0.0)
                    gp.memset(ks[j][:].bitcast(F32), 0.0)
                    gp.memset(vs[j][:, :, 0:U], 0.0)
                    gp.memset(vs[j][:, :, U + 1:C], 0.0)
                    last = gp.memset(vs[j][:, :, U:U + 1], 1.0)
                last.then_inc(fills_done, 1)
                gp.wait_ge(fills_done, 3)

                def step(stage, kind, im, place, *a):
                    if (stage, kind) == ("prepare", "pad"):
                        r, = a
                        rows = slice(r * HW // CH, (r + 1) * HW // CH)
                        cols = slice(r * S // CH, (r + 1) * S // CH)
                        wait_apart(gp, pad_hi, im.count(CH, r + 1), pool_passed)
                        gp.tensor_scalar(xin[:, cols], xin[:, cols], gs[:, 0:1], gb[:, 0:1], ALU.mult, ALU.add).then_inc(pool_chain, 1)
                        gp.wait_ge(pool_chain, im.count(CH, 1 + r))
                        inner = pad[C:P, 1 + rows.start:1 + rows.stop, 1:1 + HW]
                        gp.tensor_tensor(inner, xin[C:P, cols].rearrange("c (h w) -> c h w", w=HW), inner.bitcast(F32), ALU.subtract).then_inc(pad_lo, 1)
                        gp.wait_ge(pad_lo, im.count(CH, r + 1))
                    elif (stage, kind) == ("prepare", "var"):
                        q, = a
                        gp.wait_ge(rstd_ready, im.count(CH, q + 1))
                        gp.tensor_tensor(piece(xn, q), piece(xn, q), rstd[:, q % 2, :], ALU.mult).then_inc(xn_ready, 1)
                        gp.wait_ge(xn_ready, im.count(CH, q + 1))
                        gp.tensor_tensor(piece(base[:, im.parity, :], q), piece(tres, q), piece(xn, q), ALU.add).then_inc(base_ready, 1)
                    elif (stage, kind) == ("norms", "var"):
                        q, = a
                        gp.wait_ge(rstd2_ready, im.count(CH, q + 1))
                        gp.tensor_tensor(piece(xn2, q), piece(xn2, q), rstd2[:, q % 2, :], ALU.mult).then_inc(xn2_ready, 1)
                        gp.wait_ge(xn2_ready, im.count(CH, q + 1))
                        gp.tensor_tensor(piece(feat, q), piece(feat, q), piece(xn2, q), ALU.add).then_inc(feat_ready, 1)
                        gp.wait_ge(hi_ready, im.count(CH, q + 1))
                        if q == 0:
                            wait(gp, lo_stored, im.count(16, 0))
                        gp.tensor_tensor(piece(lo, q), piece(xn2, q), piece(hi, q).bitcast(F32), ALU.subtract).then_inc(lo_ready, 1)

                walk(gp, images, 2.2, step)

            @block1.vector
            def _(dve):
                v = nc.vector
                dve.wait_ge(fills_done, 2)
                v.memset(den_st[U:U + 1, :], 1.0)
                v.memset(den_st[C + U:C + U + 1, :], 1.0)
                for j in range(2):
                    v.memset(ks[j][KS:KS + 1, 0:S].bitcast(F32), 1.0)
                    last = v.memset(vs[j][C:P, KB - 1, :], 0.0)
                last.then_inc(fills_done, 1)
                dve.wait_ge(conv_loaded, 16)
                by_tap = conv_raw[:].rearrange("o i t -> o t i")
                v.tensor_scalar(conv_neg[:], conv_raw[:], 0.0, None, ALU.is_lt).then_inc(dve_chain, 1)
                v.tensor_scalar(conv_raw[:], conv_raw[:], 0.0, None, ALU.is_gt).then_inc(dve_chain, 1)
                dve.wait_ge(dve_chain, 2)
                for h in range(2):
                    last = v.tensor_tensor(conv_sign[:, :, h, :], by_tap, conv_neg[:].rearrange("o i t -> o t i"), ALU.subtract)
                last.then_inc(signs_ready, 1)
                dve.wait_ge(loaded_w, 16 * (3 + 2 * 10 + 2))
                v.tensor_copy(ident_r[:], ident[:]).then_inc(setup, 1)
                for tap in range(9):
                    dy, dx = tap // 3, tap % 3
                    dve.wait_ge(conv_turned, tap + 1)
                    v.tensor_copy(conv_st[:, dy, dx, 0:C], m_bank[tap % 2][:, 0:C])
                    v.tensor_copy(conv_st[:, dy + 1, dx, C:P], m_bank[tap % 2][:, 0:C]).then_inc(weights_ready, 1)

                def step(stage, kind, im, place, *a):
                    par = im.parity
                    if kind == "max":
                        b, m = a
                        dve.wait_ge(m_done, place.m(place.use + 1))
                        v.tensor_reduce(part_max[:, b, m:m + 1], m_bank[place.bank()][:, 0:MW], AX.X, ALU.max).then_inc(m_used, 1)
                    elif kind == "blockmax":
                        r, = a
                        blocks = slice(r * MR, min((r + 1) * MR, KB))
                        dve.wait_ge(m_used, place.m(place.after))
                        v.tensor_reduce(block_max[:, blocks], part_max[:, blocks, :], AX.X, ALU.max).then_inc(negmax_ready, 1)
                        dve.wait_ge(negmax_ready, im.count(2 * NMR, 2 * r + 1))
                        v.tensor_scalar(neg_max[:, KS + blocks.start:KS + blocks.stop], block_max[:, blocks], -1.0, None, ALU.mult).then_inc(negmax_ready, 1)
                    elif kind == "row":
                        r, = a
                        n0, n1 = r * MR * P, min((r + 1) * MR * P, S)
                        dve.wait_ge(m_done, place.m(place.use + 1))
                        v.tensor_copy(qs[par][KS:KS + 1, n0:n1], m_bank[place.bank()][KS:KS + 1, 0:n1 - n0]).then_inc(m_used, 1)
                    elif stage == "prepare":
                        if kind == "stats":
                            dve.wait_ge(x_loaded, im.count(32, 32))
                            for m in range(MC):
                                v.bn_stats(stats[:, m, :], xin[:, m * MW:(m + 1) * MW]).then_inc(dve_chain, 1)
                            wait_apart(dve, dve_chain, im.count(MC + 4, 2 + MC), dve_passed)
                            v.bn_aggr(mv[:], stats[:]).then_inc(dve_chain, 1)
                            dve.wait_ge(dve_chain, im.count(MC + 4, 2 + MC + 1))
                            v.tensor_copy(mv2[:, 0:1], mv[:, 0:1])
                            v.scalar_tensor_tensor(mv2[:, 1:2], mv[:, 0:1], mv[:, 0:1], mv[:, 1:2], ALU.mult, ALU.add).then_inc(moments_ready, 1)
                        elif kind == "pair":
                            dve.wait_ge(pair_done, im.count(1, 1))
                            v.tensor_copy(gm[:], x0[:, 0:2]).then_inc(dve_chain, 1)
                            dve.wait_ge(dve_chain, im.count(MC + 4, 2 + MC + 2))
                            v.tensor_tensor(gsq[:, 0:1], gm[:, 0:1], gm[:, 0:1], ALU.mult).then_inc(dve_chain, 1)
                            dve.wait_ge(dve_chain, im.count(MC + 4, 2 + MC + 3))
                            v.tensor_tensor(gvar[:, 0:1], gm[:, 1:2], gsq[:, 0:1], ALU.subtract).then_inc(gvar_ready, 1)
                        elif kind == "shift":
                            dve.wait_ge(gs_ready, im.count(1, 1))
                            v.tensor_scalar(gsq[:, 1:2], gm[:, 0:1], -1.0, None, ALU.mult).then_inc(dve_chain, 1)
                            dve.wait_ge(dve_chain, im.count(MC + 4, 2 + MC + 4))
                            v.tensor_tensor(gb[:, 0:1], gsq[:, 1:2], gs[:, 0:1], ALU.mult).then_inc(gb_ready, 1)
                        elif kind == "conv":
                            q, = a
                            if q == 0:
                                dve.wait_ge(xpk_loaded, im.count(32, 32))
                            dve.wait_ge(conv_done, im.count(CH, q + 1))
                            v.tensor_tensor(piece(tres, q), x0[:, 0:CW], piece(xpk, q), ALU.add).then_inc(tres_ready, 1)
                        elif kind == "mean":
                            q, = a
                            dve.wait_ge(mean_done, im.count(CH, q + 1))
                            v.tensor_tensor(piece(xn, q), piece(tres, q), x0[:, 0:CW], ALU.subtract).then_inc(cent_ready, 1)
                        elif kind == "proj":
                            q, n = a
                            which = (qs, ks)[n // 2][par]
                            part = slice(U, 2 * U) if n < 2 else slice(2 * U, 3 * U)
                            dst, src = proj_cols(which, part, q, n), m_bank[place.bank()][part, 0:CW]
                            if n < 2:
                                src = src.rearrange("p (c i) -> p c i", i=QW)
                            dve.wait_ge(part_hi, im.count(4 * CH, 4 * q + n + 1))
                            v.tensor_tensor(dst, src, dst.bitcast(F32), ALU.subtract).then_inc(m_used, 1)
                    elif stage == "attend" and kind == "project":
                        c, = a
                        cols = slice(c * QW, (c + 1) * QW)
                        dve.wait_ge(proj_done, im.count(QC, c + 1))
                        if c == 0 and im.c:
                            wait(dve, t2_stored, im.count(16, -16))
                        v.reciprocal(rden[:], x1[:, QW:2 * QW]).then_inc(t2_ready, 1)
                        dve.wait_ge(t2_ready, im.count(3 * QC, 3 * c + 1))
                        v.tensor_tensor(onorm[:], x1[:, 0:QW], rden[:], ALU.mult).then_inc(t2_ready, 1)
                        dve.wait_ge(t2_ready, im.count(3 * QC, 3 * c + 2))
                        v.scalar_tensor_tensor(t2[:, par, cols], onorm[:], bo_col[:, 0:1], base[:, par, cols], ALU.add, ALU.add).then_inc(t2_ready, 1)
                    elif stage == "norms" and kind == "mean":
                        q, = a
                        if q == 0:
                            wait(dve, lo_ready, im.count(CH, 0))
                        dve.wait_ge(mean2_done, im.count(CH, q + 1))
                        v.tensor_tensor(piece(xn2, q), piece(t2[:, par, :], q), x1[:, 0:CW], ALU.subtract).then_inc(cent2_ready, 1)

                walk(dve, images, 0.0, step)

            @block1.scalar
            def _(act):
                s = nc.scalar
                act.preload_act_table_set("natural_log_exp_and_others")
                act.wait_ge(fills_done, 3)

                def step(stage, kind, im, place, *a):
                    par = im.parity
                    if stage == "prepare":
                        if kind == "pair":
                            act.wait_ge(gvar_ready, im.count(1, 1))
                            s.activation(gln[:, 0:1], gvar[:, 0:1], ACT.Ln, bias=eps5[:]).then_inc(gln_ready, 1)
                            act.wait_ge(gln_ready, im.count(1, 1))
                            s.activation(gs[:, 0:1], gln[:, 0:1], ACT.Exp, scale=-0.5).then_inc(gs_ready, 1)
                        elif kind == "pad":
                            r, = a
                            if r == 0:
                                act.wait_ge(gb_ready, im.count(1, 1))
                            rows = slice(1 + r * HW // CH, 1 + (r + 1) * HW // CH)
                            cols = slice(r * S // CH, (r + 1) * S // CH)
                            s.activation(pad[:, rows, 1:1 + HW], xin[:, cols].rearrange("c (h w) -> c h w", w=HW), ACT.Identity,
                                         bias=gb[:, 0:1], scale=gs[:, 0:1]).then_inc(pad_hi, 1)
                        elif kind == "mean":
                            q, = a
                            act.wait_ge(cent_ready, im.count(CH, q + 1))
                            s.activation(sq[:, q % 2, :], piece(xn, q), ACT.Square).then_inc(sq_ready, 1)
                        elif kind == "var":
                            q, = a
                            act.wait_ge(var_done, im.count(CH, q + 1))
                            s.activation(rstd[:, q % 2, :], x0[:, 0:CW], ACT.Ln, bias=eps5[:]).then_inc(rln_ready, 1)
                            act.wait_ge(rln_ready, im.count(CH, q + 1))
                            s.activation(rstd[:, q % 2, :], rstd[:, q % 2, :], ACT.Exp, scale=-0.5).then_inc(rstd_ready, 1)
                        elif kind == "proj":
                            q, n = a
                            src = m_bank[place.bank()][0:KS, 0:CW]
                            if n < 2:
                                src = src.rearrange("p (c i) -> p c i", i=QW)
                            act.wait_ge(m_done, place.m(place.use + 1))
                            s.activation(proj_cols((qs, ks)[n // 2][par], slice(0, KS), q, n), src, ACT.Copy).then_inc(part_hi, 1)
                        elif kind == "values":
                            n, = a
                            act.wait_ge(v_done, im.count(2, n + 1))
                            b0, b1 = (0, 13) if n == 0 else (13, KB - 1)
                            last = s.activation(vs[par][:, b0:b1, 0:U], x0[:, 0:(b1 - b0) * U].rearrange("p (b u) -> p b u", u=U), ACT.Copy)
                            if n == 1:
                                last = s.activation(vs[par][0:S - b1 * P, b1, 0:U], x0[0:S - b1 * P, (b1 - b0) * U:(b1 - b0 + 1) * U], ACT.Copy)
                            last.then_inc(v_ready, 1)
                    elif stage == "attend":
                        if kind == "score":
                                c, k = a
                                n = c * KB + k
                                act.wait_ge(s_done, im.count(QC * KB, n + 1))
                                s.activation(probs[:, n % 4, :], s_bank[n % 3][:, 0:2 * QW], ACT.Exp, scale=SCALE).then_inc(p_ready, 1)
                        elif kind == "gather":
                            c, = a
                            act.wait_ge(o_done, im.count(QC, c + 1))
                            s.activation(osb[:, c % 2, :], o_bank[:, 0:2 * QW], ACT.Copy).then_inc(o_saved, 1)
                    elif stage == "norms":
                        q, = a
                        if kind == "mean":
                            act.wait_ge(cent2_ready, im.count(CH, q + 1))
                            s.activation(sq2[:, q % 2, :], piece(xn2, q), ACT.Square).then_inc(sq2_ready, 1)
                        elif kind == "var":
                            act.wait_ge(var2_done, im.count(CH, q + 1))
                            s.activation(rstd2[:, q % 2, :], x1[:, 0:CW], ACT.Ln, bias=eps5[:]).then_inc(rln2_ready, 1)
                            act.wait_ge(rln2_ready, im.count(CH, q + 1))
                            s.activation(rstd2[:, q % 2, :], rstd2[:, q % 2, :], ACT.Exp, scale=-0.5).then_inc(rstd2_ready, 1)
                        elif kind == "hi":
                            act.wait_ge(xn2_ready, im.count(CH, q + 1))
                            if q == 0:
                                wait(act, hi_stored, im.count(16, 0))
                            s.activation(piece(hi, q), piece(xn2, q), ACT.Copy).then_inc(hi_ready, 1)

                walk(act, images, 2.2, step)

            @block1.tensor
            def _(pe):
                mm = nc.tensor.matmul
                pe.wait_ge(loaded_w, 16 * (3 + 2 * 10 + 2))
                pe.wait_ge(signs_ready, 1)
                for tap in range(9):
                    if tap >= 2:
                        pe.wait_ge(weights_ready, tap - 1)
                    mm(m_bank[tap % 2][:, 0:C], conv_sign[:, tap, :, :].rearrange("o h i -> o (h i)"), ident[0:C, 0:C], start=True, stop=True).then_inc(conv_turned, 1)
                pe.wait_ge(weights_ready, 9)
                pe.wait_ge(setup, 1)

                def step(stage, kind, im, place, *a):
                    par = im.parity
                    if kind == "max":
                        b, m = a
                        if (b, m) == (0, 0):
                            pe.wait_ge(m_used, place.m(place.use))
                        wait(pe, m_used, place.m(place.use - 1))
                        mm(m_bank[place.bank()][:, 0:MW], qs[par][0:KS, b * P:(b + 1) * P], ks[par][0:KS, m * MW:(m + 1) * MW], start=True, stop=True).then_inc(m_done, 1)
                    elif kind == "row":
                        r, = a
                        pe.wait_ge(negmax_ready, im.count(2 * NMR, 2 * r + 2))
                        wait(pe, m_used, place.m(place.use - 1))
                        for b in range(r * MR, min((r + 1) * MR, KB)):
                            last = mm(m_bank[place.bank()][0:KS + 1, b % MR * P:(b % MR + 1) * P], neg_max[:, b:b + KS + 1], ident_r[:], start=True, stop=True)
                        last.then_inc(m_done, 1)
                    elif stage == "attend":
                        if kind == "score":
                            c, k = a
                            if k == 0:
                                wait(pe, m_used, place.m(place.after))
                            if k % 2 and k >= 3:
                                pe.wait_ge(p_ready, im.count(QC * KB, c * KB + k - 2))
                            mm(s_bank[(c * KB + k) % 3][:, 0:2 * QW], ks[par][0:KS + 1, k * P:(k + 1) * P], qs[par][0:KS + 1, c * 2 * QW:(c + 1) * 2 * QW],
                               start=True, stop=True).then_inc(s_done, 1)
                        elif kind == "value":
                            c, k = a
                            if k == 0:
                                wait(pe, o_saved, im.count(QC, c))
                            pe.wait_ge(p_ready, im.count(QC * KB, c * KB + min(k + 2, KB)))
                            for h in range(2):
                                half = slice(h * C, (h + 1) * C)
                                if k + 1 < KB:
                                    mm(o_bank[half, 0:2 * QW], vs[par][:, k + h, :], probs[:, (c * KB + k + h) % 4, :], start=k == 0, stop=False)
                                else:
                                    last = mm(o_bank[half, h * QW:(h + 1) * QW], vs[par][:, k, :], probs[:, (c * KB + k) % 4, h * QW:(h + 1) * QW], start=False, stop=True)
                            if k + 1 == KB:
                                last.then_inc(o_done, 1)
                        elif kind == "project":
                            c, = a
                            pe.wait_ge(o_saved, im.count(QC, c + 1))
                            if c == 0:
                                wait(pe, rln2_ready, im.count(CH, 0))
                            else:
                                pe.wait_ge(t2_ready, im.count(3 * QC, 3 * c - 1))
                            for n, weights in enumerate((wo_st, den_st)):
                                for h in range(2):
                                    last = mm(x1[h * C:(h + 1) * C, n * QW:(n + 1) * QW], weights[:], osb[:, c % 2, h * QW:(h + 1) * QW], start=True, stop=True)
                            last.then_inc(proj_done, 1)
                    elif stage == "norms":
                        q, = a
                        if kind == "mean":
                            if q == 0:
                                pe.wait_ge(t2_ready, im.count(3 * QC, 3 * QC))
                            elif q == 1:
                                pe.wait_ge(cent2_ready, im.count(CH, 1))
                            else:
                                pe.wait_ge(rln2_ready, im.count(CH, q - 1))
                            mm(x1[:, 0:CW], block[:], piece(t2[:, par, :], q), start=True, stop=True).then_inc(mean2_done, 1)
                        elif kind == "var":
                            if q < 3:
                                pe.wait_ge(cent2_ready, im.count(CH, q + 2))
                            else:
                                pe.wait_ge(rln2_ready, im.count(CH, 3))
                            pe.wait_ge(sq2_ready, im.count(CH, q + 1))
                            mm(x1[:, 0:CW], block[:], sq2[:, q % 2, :], start=True, stop=True).then_inc(var2_done, 1)
                    elif kind == "pair":
                        pe.wait_ge(moments_ready, im.count(1, 1))
                        wait(pe, v_ready, im.count(2, 0))
                        mm(x0[:, 0:2], pair[:], mv2[:], start=True, stop=True).then_inc(pair_done, 1)
                    elif kind == "conv":
                        q, = a
                        pe.wait_ge(pad_lo, im.count(CH, min(q + 2, CH)))
                        if q == 0:
                            pe.wait_ge(gvar_ready, im.count(1, 1))
                        else:
                            pe.wait_ge(cent_ready, im.count(CH, q))
                        for r in range(4):
                            for dx in range(3):
                                top = 2 * CP * q + r
                                last = mm(x0[:, 0:CW].rearrange("p (r w) -> p r w", w=HW), conv_st[:, r, dx, :],
                                          pad[:, top:top + 2 * CP - 1:2, dx:dx + HW], start=r + dx == 0, stop=r + dx == 5)
                        last.then_inc(conv_done, 1)
                    elif kind == "mean":
                        q, = a
                        pe.wait_ge(tres_ready, im.count(CH, q + 1))
                        if q:
                            pe.wait_ge(rln_ready, im.count(CH, q))
                        mm(x0[:, 0:CW], block[:], piece(tres, q), start=True, stop=True).then_inc(mean_done, 1)
                    elif kind == "var":
                        q, = a
                        if q < 3:
                            pe.wait_ge(tres_ready, im.count(CH, q + 2))
                        else:
                            pe.wait_ge(cent_ready, im.count(CH, CH))
                        pe.wait_ge(sq_ready, im.count(CH, q + 1))
                        mm(x0[:, 0:CW], block[:], sq[:, q % 2, :], start=True, stop=True).then_inc(var_done, 1)
                    elif kind == "proj":
                        q, n = a
                        if n == 0:
                            pe.wait_ge(xn_ready, im.count(CH, q + 1))
                        wait(pe, m_used, place.m(place.use - 1))
                        h, weights = n % 2, (wq_st, wk_st)[n // 2]
                        rows = slice(h * C, (h + 1) * C)
                        mm(m_bank[place.bank()][:, 0:CW], weights[rows].rearrange("p r u -> p (r u)"), xn[rows, q * CW:(q + 1) * CW], start=True, stop=True).then_inc(m_done, 1)
                    elif kind == "values":
                        n, = a
                        if n == 0:
                            pe.wait_ge(xn_ready, im.count(CH, CH))
                            pe.wait_ge(rln_ready, im.count(CH, CH))
                        else:
                            pe.wait_ge(v_ready, im.count(2, 1))
                        b0, b1 = (0, 13) if n == 0 else (13, KB)
                        for b in range(b0, b1):
                            at, end = b * P, min((b + 1) * P, S)
                            while at < end:
                                h, row = at // HALF, at % P
                                stop = min(end, (h + 1) * HALF, at + (P if row == 0 else 64 if row == 64 else 32))
                                last = mm(x0[row:row + stop - at, (b - b0) * U:(b - b0 + 1) * U], xn[h * C:(h + 1) * C, at - h * HALF:stop - h * HALF],
                                          wv_st[h * C:(h + 1) * C, :], start=True, stop=True)
                                at = stop
                        last.then_inc(v_done, 1)

                walk(pe, images, 0.0, step)


def rows_of(w):
    return w.rearrange("(e a) h k -> a h e k", a=2)


def expert_phase(nc, images, w_r, b_r, w1, b1, g1, be1, m1, v1, w2, b2, g2, be2, m2, v2, w3, b3, select_in,
                 t2_dram, hi_dram, lo_dram, out, ident, feat):
    out_rows = out.rearrange("i c (r a) w -> i a c r w", a=2)
    groups = images // 4
    ctx = ExitStack()
    with ctx:
        def sb(name, shape, dt=F32):
            return ctx.enter_context(nc.sbuf_tensor(name, shape, dt))

        def sem(name):
            return ctx.enter_context(nc.semaphore(name))

        eps3 = sb("eps3", [P, 1])
        select = sb("select", [EXP, EP, P])
        w1f = sb("w1f", [P, EXP * HID])
        w1h, w1l = sb("w1h", [P, EXP * HID], F32R), sb("w1l", [P, EXP * HID], F32R)
        w2f = sb("w2f", [P, EP, P])
        w3f = sb("w3f", [P, EP, C])
        g2row, v2row, r2row, s2row = (sb(n, [P, EXP * HID]) for n in ("g2row", "v2row", "r2row", "s2row"))
        cols = {n: sb("col_" + n, [P, EP]) for n in ("b1", "g1", "be1", "m1", "v1", "b2", "g2", "be2", "m2", "v2")}
        tmp = {n: sb("tmp_" + n, [P, EP]) for n in ("l1", "r1", "s1", "d1", "p1", "c1", "l2", "r2", "s2", "d2", "p2", "c2", "n2")}
        c2_st = sb("c2_st", [P, EP, EXP])
        b3f, b3w = sb("b3f", [EXP, C]), sb("b3w", [EXP, 2, C])
        wr_sb, br_row = sb("wr_sb", [P, EXP]), sb("br_row", [P, EXP])
        NB = 2 * RB
        logits, shifted, powers, gates = (sb(n, [P, NB, EXP]) for n in ("logits", "shifted", "powers", "gates"))
        top, total, inverse = sb("top", [P, NB]), sb("total", [P, NB]), sb("inverse", [P, NB])
        gates_t = sb("gates_t", [EXP, 2 * RW])
        gate_w = sb("gate_w", [P, EP, CW])
        bias_w = sb("bias_w", [P, CW])
        xs = sb("xs", [P, 4, CW], F32R)
        res = sb("res", [P, 2, CW])
        h1, h2 = sb("h1", [P, 2, 2, CW]), sb("h2", [P, 2, 2, CW])
        fin = sb("fin", [P, 2, CW])
        pb = [ctx.enter_context(nc.psum_tensor(f"ebank{j}", [P, 2, 512], F32)) for j in range(4)]
        bank1, bank2, bank3, bank4 = pb

        loaded, filled, cols_ready, row_ready, chain, w_ready = (sem(n) for n in ("loaded2", "filled2", "cols_ready", "rows_ready2", "chain2", "w_ready2"))
        c2_ready, b3_done, logits_done, shift_ready, powers_ready, gates_ready, turned, turn_saved = (
            sem(n) for n in ("c2_ready", "b3_done", "logits_done", "shift_ready", "powers_ready", "gates_ready", "turned", "turn_saved"))
        half_done = sem("half_done")
        gate_done, gate_saved, gate_passed = sem("gate_done"), sem("gate_saved"), sem("gate_passed")
        xs_loaded, res_loaded, res_ready = sem("xs_loaded"), sem("res_loaded"), sem("res_ready")
        a_done, a_half, h1_ready, b_done, h2_ready, c_done, fin_ready, stored = (
            sem(n) for n in ("a_done", "a_half", "h1_ready", "b_done", "h2_ready", "c_done", "fin_ready", "out_stored"))

        TURN_BANKS = -(-NB // 4)
        with nc.Block() as block2:
            @block2.sync
            def _(sp):
                def load(dst, src):
                    sp.dma_start(dst, src).then_inc(loaded, 16)
                load(select[:], select_in)
                for h in range(2):
                    load(w1f[h * C:(h + 1) * C, :].rearrange("d (e h) -> d e h", h=HID), w1.rearrange("e d h -> d e h"))
                    load(wr_sb[h * C:(h + 1) * C, :], w_r)
                    load(w3f[h * C:(h + 1) * C, :, :], rows_of(w3)[h])
                    for name, src in (("b1", b1), ("g1", g1), ("be1", be1), ("m1", m1), ("v1", v1), ("b2", b2), ("g2", g2), ("be2", be2), ("m2", m2), ("v2", v2)):
                        sp.dma_start(cols[name][h * C:(h + 1) * C, :], src.rearrange("(e a) h -> a h e", a=2)[h], allow_slow_non_contiguous=True).then_inc(loaded, 16)
                load(b3f[:], b3)
                load(br_row[:], b_r.partition_broadcast(P))
                load(g2row[:], g2.rearrange("e k -> (e k)").partition_broadcast(P))
                load(v2row[:], v2.rearrange("e k -> (e k)").partition_broadcast(P))
                sp.wait_ge(filled, 1)
                for h in range(2):
                    load(w2f[h * C:(h + 1) * C, :, h * HID:(h + 1) * HID], rows_of(w2)[h])
            LOADS = 16 * (1 + 2 * 13 + 4 + 2)

            @block2.gpsimd
            def _(gp):
                gp.memset(w2f[:], 0.0).then_inc(filled, 1)
                gp.memset(c2_st[:], 0.0)
                gp.memset(eps3[:], 1e-3).then_inc(filled, 1)

            @block2.scalar
            def _(act):
                s = nc.scalar
                act.preload_act_table_set("natural_log_exp_and_others")
                act.wait_ge(loaded, LOADS)
                act.wait_ge(filled, 2)
                s.activation(tmp["l1"][:], cols["v1"][:], ACT.Ln, bias=eps3[:])
                s.activation(tmp["l2"][:], cols["v2"][:], ACT.Ln, bias=eps3[:])
                s.activation(r2row[:], v2row[:], ACT.Ln, bias=eps3[:]).then_inc(row_ready, 1)
                act.wait_ge(row_ready, 1)
                s.activation(tmp["r1"][:], tmp["l1"][:], ACT.Exp, scale=-0.5)
                s.activation(tmp["r2"][:], tmp["l2"][:], ACT.Exp, scale=-0.5)
                s.activation(s2row[:], r2row[:], ACT.Exp, scale=-0.5).then_inc(row_ready, 1)
                act.wait_ge(shift_ready, 1)
                s.activation(powers[:], shifted[:], ACT.Exp).then_inc(powers_ready, 1)

            @block2.vector
            def _(dve):
                v = nc.vector
                links = [0]

                def link(ins):
                    links[0] += 1
                    ins.then_inc(chain, 1)
                    dve.wait_ge(chain, links[0])

                dve.wait_ge(loaded, LOADS)
                dve.wait_ge(filled, 2)
                link(v.tensor_copy(w1h[:], w1f[:]))
                v.tensor_tensor(w1l[:], w1f[:], w1h[:].bitcast(F32), ALU.subtract)
                dve.wait_ge(row_ready, 2)
                for n in "12":
                    v.tensor_tensor(tmp["s" + n][:], cols["g" + n][:], tmp["r" + n][:], ALU.mult)
                    link(v.tensor_tensor(tmp["d" + n][:], cols["b" + n][:], cols["m" + n][:], ALU.subtract))
                    link(v.tensor_tensor(tmp["p" + n][:], tmp["d" + n][:], tmp["s" + n][:], ALU.mult))
                    link(v.tensor_tensor(tmp["c" + n][:], tmp["p" + n][:], cols["be" + n][:], ALU.add))
                v.tensor_scalar(tmp["n2"][:], tmp["c2"][:], -1.0, None, ALU.mult)
                link(v.tensor_tensor(s2row[:], s2row[:], g2row[:], ALU.mult))
                v.tensor_tensor(w2f[:], w2f[:], s2row[:].rearrange("p (e m) -> p e m", e=EP), ALU.mult)
                for e in range(EXP):
                    rows = slice((e % 2) * HID, (e % 2 + 1) * HID)
                    last = v.tensor_copy(c2_st[rows, e // 2, e:e + 1], tmp["c2"][rows, e // 2:e // 2 + 1])
                last.then_inc(c2_ready, 1)
                dve.wait_ge(b3_done, 1)
                v.tensor_tensor(b3w[:, 0, :], bank4[0:EXP, 0, 0:C], b3f[:], ALU.add)
                v.tensor_tensor(b3w[:, 1, :], bank4[0:EXP, 0, 0:C], b3f[:], ALU.add)
                dve.wait_ge(logits_done, 1)
                link(v.scalar_tensor_tensor(logits[:], bank4[:, 1, 0:NB * EXP].rearrange("p (b e) -> p b e", e=EXP), 1.0 / images,
                                            br_row[:].rearrange("p (b e) -> p b e", b=1).broadcast_to([P, NB, EXP]), ALU.mult, ALU.add))
                link(v.tensor_reduce(top[:], logits[:], AX.X, ALU.max))
                v.tensor_tensor(shifted[:], logits[:], top[:].rearrange("p (b e) -> p b e", e=1).broadcast_to([P, NB, EXP]), ALU.subtract).then_inc(shift_ready, 1)
                dve.wait_ge(powers_ready, 1)
                link(v.tensor_reduce(total[:], powers[:], AX.X, ALU.add))
                link(v.reciprocal(inverse[:], total[:]))
                v.tensor_tensor(gates[:], powers[:], inverse[:].rearrange("p (b e) -> p b e", e=1).broadcast_to([P, NB, EXP]), ALU.mult).then_inc(gates_ready, 1)
                for n in range(TURN_BANKS):
                    b1_, b0_ = min(4 * n + 4, NB), 4 * n
                    dve.wait_ge(turned, n + 1)
                    v.tensor_copy(gates_t[:, b0_ * P:b1_ * P], bank3[0:EXP, n % 2, 0:(b1_ - b0_) * P]).then_inc(turn_saved, 1)

            @block2.tensor
            def _(pe):
                mm = nc.tensor.matmul
                pe.wait_ge(c2_ready, 1)
                for e in range(EP):
                    last = mm(bank4[0:EXP, 0, 0:C], c2_st[:, e, :], w3f[:, e, :], start=e == 0, stop=e == EP - 1)
                last.then_inc(b3_done, 1)
                for b in range(NB):
                    if b == RB:
                        last.then_inc(half_done, 1)
                        pe.wait_ge(half_done, 1)
                    rows = slice(b // RB * C, (b // RB + 1) * C)
                    at = b % RB * P
                    last = mm(bank4[:, 1, b * EXP:(b + 1) * EXP], feat[rows, at:at + P], wr_sb[rows, :], start=True, stop=True)
                last.then_inc(logits_done, 1)
                pe.wait_ge(gates_ready, 1)
                for n in range(TURN_BANKS):
                    if n >= 2:
                        pe.wait_ge(turn_saved, n - 1)
                    for b in range(4 * n, min(4 * n + 4, NB)):
                        last = mm(bank3[0:EXP, n % 2, b % 4 * P:(b % 4 + 1) * P], gates[:, b, :], ident[:], start=True, stop=True)
                    last.then_inc(turned, 1)

        class Turn:

            def __init__(self, half, r, g=0):
                self.half, self.r, self.g = half, r, g

            def count(self, per, n):
                return self.half * (CH * groups * per) + self.r * (groups * per) + self.g * per + n

            def block_count(self, per, n):
                return self.half * (CH * per) + self.r * per + n

        def turns(engine, prologue, body):
            with engine.Fori(0, 2) as half:
                with engine.Fori(0, CH) as r:
                    if prologue is not None:
                        prologue(Turn(half, r))
                    with engine.Fori(0, groups) as g:
                        body(Turn(half, r, g))

        def part(dram, turn, j):
            return dram[bass.ds(turn.g * 4 + j, 1), bass.ds(turn.half, 1), :, bass.ds(turn.r * CW, CW)].rearrange("i a c n -> (i a c) n")

        with nc.Block() as block3:
            @block3.sync
            def _(sp):
                def body(turn):
                    for p in range(2):
                        sp.wait_ge(a_done, turn.count(2, p))
                        for j in (2 * p, 2 * p + 1):
                            sp.dma_start(xs[0:C, j, :].bitcast(F32), part(hi_dram, turn, j)).then_inc(xs_loaded, 16)
                            sp.dma_start(xs[C:P, j, :].bitcast(F32), part(lo_dram, turn, j)).then_inc(xs_loaded, 16)
                        sp.wait_ge(fin_ready, turn.count(2, p))
                        for h in range(2):
                            sp.dma_start(res[h * C:(h + 1) * C, p, :], part(t2_dram, turn, 2 * p + h)).then_inc(res_loaded, 16)
                turns(sp, None, body)

            @block3.gpsimd
            def _(gp):
                def body(turn):
                    for p in range(2):
                        gp.wait_ge(res_loaded, turn.count(64, 32 * (p + 1)))
                        if p == 0:
                            gp.wait_ge(gate_saved, turn.block_count(EP + 1, EP + 1))
                        gp.tensor_tensor(res[:, p, :], res[:, p, :], bias_w[:], ALU.add).then_inc(res_ready, 1)
                    for p in range(2):
                        gp.wait_ge(fin_ready, turn.count(2, p + 1))
                        for h in range(2):
                            dst = out_rows[bass.ds(turn.g * 4 + 2 * p + h, 1), bass.ds(turn.half, 1), :, bass.ds(turn.r * CP, CP), :]
                            gp.dma_start(dst.rearrange("i a c r w -> (i a c) r w"), fin[h * C:(h + 1) * C, p, :].rearrange("c (r w) -> c r w", w=HW)).then_inc(stored, 16)
                turns(gp, None, body)
                gp.wait_ge(stored, 16 * 2 * 2 * 2 * CH * groups)

            @block3.scalar
            def _(act):
                s = nc.scalar

                def prologue(turn):
                    act.wait_ge(fin_ready, turn.block_count(2 * groups, 0))
                    act.wait_ge(res_ready, turn.block_count(2 * groups, 0))
                    for e in range(EP + 1):
                        act.wait_ge(gate_done, turn.block_count(EP + 1, e + 1))
                        s.activation(gate_w[:, e, :] if e < EP else bias_w[:], bank4[:, e % 2, 0:CW], ACT.Copy).then_inc(gate_saved, 1)

                def body(turn):
                    for n in range(2 * EP):
                        act.wait_ge(a_half, turn.count(2 * EP, n + 1))
                        e = n % EP
                        s.activation(h1[:, n % 2, :, :], bank1[:, :, 0:CW], ACT.Relu, bias=tmp["c1"][:, e:e + 1], scale=tmp["s1"][:, e:e + 1]).then_inc(h1_ready, 1)
                turns(act, prologue, body)

            @block3.vector
            def _(dve):
                v = nc.vector

                def body(turn):
                    for n in range(2 * EP):
                        p, e = n // EP, n % EP
                        if n == 0:
                            dve.wait_ge(gate_saved, turn.block_count(EP + 1, EP))
                        dve.wait_ge(b_done, turn.count(2 * EP, n + 1))
                        v.scalar_tensor_tensor(h2[:, n % 2, :, :], bank2[:, :, 0:CW], tmp["n2"][:, e:e + 1],
                                               gate_w[:, e:e + 1, :].broadcast_to([P, 2, CW]), ALU.max, ALU.mult).then_inc(h2_ready, 1)
                        if n == EP or n == 2 * EP - 1:
                            finish(turn, (n - 1) // EP if n == EP else 1)

                def finish(turn, p):
                    dve.wait_ge(c_done, turn.count(2, p + 1))
                    dve.wait_ge(res_ready, turn.count(2, p + 1))
                    if p == 0:
                        dve.wait_ge(stored, turn.count(64, 0))
                    v.tensor_tensor(fin[:, p, :], bank3[:, p, 0:CW], res[:, p, :], ALU.add).then_inc(fin_ready, 1)
                turns(dve, None, body)

            @block3.tensor
            def _(pe):
                mm = nc.tensor.matmul

                def prologue(turn):
                    for e in range(EP + 1):
                        wait_apart(pe, gate_saved, turn.block_count(EP + 1, max(e - 1, 0)), gate_passed)
                        weights = select[:, e, :] if e < EP else b3w[:].rearrange("e a c -> e (a c)")
                        mm(bank4[:, e % 2, 0:CW], weights, gates_t[:, bass.ds(turn.half * RW + turn.r * CW, CW)], start=True, stop=True).then_inc(gate_done, 1)

                def body(turn):
                    for n in range(2 * EP + 2):
                        if n < 2 * EP:
                            p, e = n // EP, n % EP
                            if e == 0:
                                pe.wait_ge(xs_loaded, turn.count(128, 64 * (p + 1)))
                            pe.wait_ge(h1_ready, turn.count(2 * EP, n))
                            for j in range(2):
                                mm(bank1[:, j, 0:CW], w1h[:, e * P:(e + 1) * P], xs[:, 2 * p + j, :], start=True, stop=False)
                                last = mm(bank1[:, j, 0:CW], w1l[:, e * P:(e + 1) * P], xs[:, 2 * p + j, :], start=False, stop=True)
                            last.then_inc(a_half, 1)
                            if e == EP - 1:
                                pe.wait_ge(a_half, turn.count(2 * EP, n + 1))
                                pe.sem_inc(a_done, 1)
                        if 1 <= n <= 2 * EP:
                            m = n - 1
                            pe.wait_ge(h1_ready, turn.count(2 * EP, m + 1))
                            pe.wait_ge(h2_ready, turn.count(2 * EP, m))
                            for j in range(2):
                                last = mm(bank2[:, j, 0:CW], w2f[:, m % EP, :], h1[:, m % 2, j, :], start=True, stop=True)
                            last.then_inc(b_done, 1)
                        if n >= 2:
                            m = n - 2
                            p, e = m // EP, m % EP
                            if e == 0:
                                pe.wait_ge(fin_ready, turn.count(2, p))
                            pe.wait_ge(h2_ready, turn.count(2 * EP, m + 1))
                            for j in range(2):
                                last = mm(bank3[j * C:(j + 1) * C, p, 0:CW], w3f[:, e, :], h2[:, m % 2, j, :], start=e == 0, stop=e == EP - 1)
                            if e == EP - 1:
                                last.then_inc(c_done, 1)
                turns(pe, prologue, body)


def build(nc, images, x, conv_w, w_q, w_k, w_v, w_o, b_o, w_r, b_r, w1, b1, g1, be1, m1, v1,
          w2, b2, g2, be2, m2, v2, w3, b3, ident_in, block_in, pair_in, select_in, out):
    t2_dram = nc.dram_tensor("t2_dram", (images, 2, C, HALF), F32).ap()
    hi_dram = nc.dram_tensor("hi_dram", (images, 2, C, HALF), F32).ap()
    lo_dram = nc.dram_tensor("lo_dram", (images, 2, C, HALF), F32).ap()
    with nc.sbuf_tensor("ident", [P, P], F32) as ident, nc.sbuf_tensor("feat", [P, RW], F32) as feat:
        attention_phase(nc, images, x, conv_w, w_q, w_k, w_v, w_o, b_o, ident_in, block_in, pair_in, t2_dram, hi_dram, lo_dram, ident, feat)
        expert_phase(nc, images, w_r, b_r, w1, b1, g1, be1, m1, v1, w2, b2, g2, be2, m2, v2, w3, b3, select_in,
                     t2_dram, hi_dram, lo_dram, out, ident, feat)


INPUTS = ["x", "L0_conv_weight", "L1_attn_W_q", "L1_attn_W_k", "L1_attn_W_v", "L1_attn_W_o", "L1_attn_b_o", "L1_ffn_Wr", "L1_ffn_br",
          "L1_ffn_W1", "L1_ffn_b1", "L1_ffn_g1", "L1_ffn_be1", "L1_ffn_m1", "L1_ffn_v1",
          "L1_ffn_W2", "L1_ffn_b2", "L1_ffn_g2", "L1_ffn_be2", "L1_ffn_m2", "L1_ffn_v2", "L1_ffn_Wo", "L1_ffn_bo"]


def constants():
    n = np.arange(P)
    ident = np.eye(P, dtype=np.float32)
    block = (n[:, None] // C == n[None, :] // C).astype(np.float32) / C
    pair = (n[:, None] // 2 == n[None, :] // 2).astype(np.float32) / 2
    expert = 2 * np.arange(EP)[:, None] + n[None, :] // HID
    select = (np.arange(EXP)[:, None, None] == expert[None]).astype(np.float32)
    return {"ident": ident, "block": block, "pair": pair, "select": select}


def kernel(**inputs):
    import concourse.bacc as bacc
    from concourse.bass_utils import run_bass_kernel_spmd

    nc = bacc.Bacc("TRN2", target_bir_lowering=False, num_devices=1)
    arrays, args = {}, []
    for name, a in [(n, inputs[n]) for n in INPUTS] + list(constants().items()):
        a = np.ascontiguousarray(a)
        arrays[f"in_{name}_dram"] = a
        args.append(nc.dram_tensor(f"in_{name}_dram", a.shape, F32, kind="ExternalInput").ap())
    shape = tuple(inputs["x"].shape)
    out = nc.dram_tensor("out_dram", shape, F32, kind="ExternalOutput").ap()
    build(nc, shape[0], *args, out)
    result = run_bass_kernel_spmd(nc, [arrays], core_ids=[0])
    return result.results[0]["out_dram"]
```

```python
import numpy as np
import concourse.bass as bass
from concourse import mybir
from contextlib import ExitStack

F32, F32R = mybir.dt.float32, mybir.dt.float32r
ALU, ACT, AX = mybir.AluOpType, mybir.ActivationFunctionType, mybir.AxisListType

P = 128
C = 64
HW = 56
PAIRS = HW // 2
HALF = PAIRS * HW
S = 2 * HALF
U = 32
HID, EXP = 64, 8
EP = EXP // 2
CH = 4
CW = HALF // CH
CP = PAIRS // CH
QC = 8
QW = HALF // QC
KB = -(-S // P)
SP = KB * P
MC = 7
MW = S // MC
KS = 3 * U
MR = 4
NMR = -(-KB // MR)
AHEAD = 5
PADW = HW + 2
RB = -(-HALF // P)
RW = RB * P
SCALE = 1.0 / float(np.sqrt(U))

N_M0 = 4 * CH + AHEAD * MR * MC + AHEAD
N_M = 4 * CH + KB * MC + NMR
STEPS = KB + 1
SLOT = QC * STEPS
DVE_LAG = 0.3
VALUE_AFTER = 3.1
PIECE_STEP = 3
NORM_STEP = 2.5
PROJ_STEP = 2
PROJECT_AT = 4
DIVIDE_STEP = 1.4
CONV_AT, NORMS_AT, STATS_AT = 3, 10, 85


def timeline(lag):
    order = []
    for c in range(QC):
        for k in range(0, KB, 2):
            order.append((c * STEPS + k, "attend", "score", (c, k)))
            if k + 1 < KB:
                order.append((c * STEPS + k + 1, "attend", "score", (c, k + 1)))
            order.append((c * STEPS + k + VALUE_AFTER, "attend", "value", (c, k)))
        end, stage = ((c + 1) * STEPS, "attend") if c + 1 < QC else (0, "norms")
        order.append((end + 1.5, stage, "gather", (c,)))
        order.append((end + PROJECT_AT + lag, stage, "project", (c,)))
        order += [(end + PROJECT_AT + 1 + DIVIDE_STEP * n + lag, stage, "divide", (c, n)) for n in range(4)]
    at = NORMS_AT
    for kind, q in (("mean", 0), ("mean", 1), ("var", 0), ("mean", 2), ("var", 1), ("mean", 3), ("var", 2), ("var", 3)):
        order.append((at + lag, "norms", kind, (q,)))
        if kind == "var":
            order.append((at + 5 + lag, "norms", "hi", (q,)))
        at += NORM_STEP
    order += [(STATS_AT + 2.5 * m, "normalize", "stats", (m,)) for m in range(MC)]
    at = STATS_AT + 2.5 * MC
    order += [(at + 1, "normalize", "moments", ()), (at + 5 + lag, "normalize", "pair", ()), (at + 8 + lag, "normalize", "shift", ())]
    order += [(at + 12 + 4 * r + lag, "normalize", "pad", (r,)) for r in range(CH)]
    at = CONV_AT
    for kind, q in (("conv", 0), ("mean", 0), ("conv", 1), ("var", 0), ("mean", 1), ("conv", 2), ("var", 1), ("mean", 2),
                    ("conv", 3), ("var", 2), ("mean", 3), ("var", 3)):
        order.append((at + lag, "prepare", kind, (q,)))
        if kind == "var":
            order += [(at + 7 + PROJ_STEP * n, "prepare", "proj", (q, n)) for n in range(4)]
        at += PIECE_STEP
    order += [(at + 5 + 3 * n + lag, "prepare", "values", (n,)) for n in range(2)]
    border = at + 12
    ahead = AHEAD * MR
    for b in range(KB):
        start, blocks, places, stage = (border, ahead, SLOT - 6 - border, "prepare") if b < ahead else (0.5, KB - ahead, border - 6, "attend")
        for m in range(MC):
            place = start + (b % ahead * MC + m) * places / (blocks * MC)
            order.append((place, stage, "max", (b, m)))
        if b % MR == MR - 1 or b == KB - 1:
            order.append((place + 1.3, stage, "blockmax", (b // MR,)))
            order.append((place + 2.6, stage, "negate", (b // MR,)))
            order.append((place + 4.2, stage, "row", (b // MR,)))
    return sorted(order, key=lambda entry: entry[0])


def rows_needed(c):
    return -(-(c + 1) * 2 * QW // (P * MR))


class Place:

    def __init__(self, slot, use, after):
        self.slot, self.use, self.after = slot, use, after

    def m(self, n):
        return n if self.slot is None else self.slot.count(N_M, N_M0 + n)

    def bank(self):
        return (self.use + (0 if self.slot is None else self.slot.c * N_M + N_M0)) % 2


class Image:

    def __init__(self, c, t=None):
        self.c, self.t, self.parity = c, t, c % 2

    def count(self, per, n):
        return self.c * per + n if self.t is None else self.t * (2 * per) + (self.c * per + n)

    def number(self):
        return self.c if self.t is None else self.t * 2 + self.c


def wait(engine, semaphore, value):
    if not isinstance(value, int) or value > 0:
        engine.wait_ge(semaphore, value)


def wait_apart(engine, semaphore, value, passed):
    wait(engine, semaphore, value)
    engine.sem_inc(passed, 1)


ACT_LAG = 0.8
def walk(engine, images, lag, step):
    order = timeline(lag)

    def slot(normalize, prepare, attend, norms):
        stages = {"normalize": normalize, "prepare": prepare, "attend": attend, "norms": norms}
        uses, after = {}, {}
        for _, stage, kind, args in order:
            if stages[stage] is not None:
                if kind in ("proj", "max", "row"):
                    uses[kind, args] = len(uses)
                elif kind == "blockmax":
                    after[kind, args] = uses["max", (min(args[0] * MR + MR, KB) - 1, MC - 1)] + 1
                elif kind == "score" and args[1] == 0:
                    needed = rows_needed(args[0]) - 1
                    after[kind, args] = 0 if needed < AHEAD else uses["row", (needed,)] + 1
        at = attend if attend is not None else norms
        for _, stage, kind, args in order:
            if stages[stage] is not None:
                place = Place(None if attend is None and norms is None else at, uses.get((kind, args)), after.get((kind, args)))
                step(stage, kind, stages[stage], place, *args)

    slot(Image(0), None, None, None)
    slot(Image(1), Image(0), None, None)
    slot(Image(2), Image(1), Image(0), None)
    loops = (images - 4) // 2
    with engine.Fori(0, loops) as t:
        for j in range(2):
            slot(Image(j + 3, t), Image(j + 2, t), Image(j + 1, t), Image(j, t))
    slot(Image(images - 1), Image(images - 2), Image(images - 3), Image(images - 4))
    slot(None, Image(images - 1), Image(images - 2), Image(images - 3))
    slot(None, None, Image(images - 1), Image(images - 2))
    slot(None, None, None, Image(images - 1))


def attention_phase(nc, images, x, conv_w, w_q, w_k, w_v, w_o, b_o, ident_in, block_in, pair_in, t2_dram, hi_dram, lo_dram, ident, feat):
    x_rows = x.rearrange("i c (r a) w -> i a c r w", a=2)
    x_flat = x.rearrange("i c h w -> i c (h w)")

    ctx = ExitStack()
    with ctx:
        def sb(name, shape, dt=F32):
            return ctx.enter_context(nc.sbuf_tensor(name, shape, dt))

        def sem(name):
            return ctx.enter_context(nc.semaphore(name))

        block, pair = sb("block", [P, P]), sb("pair", [P, P])
        ident_r = sb("ident_r", [P, P], F32R)
        eps5 = sb("eps5", [P, 1])
        conv_raw = sb("conv_raw", [C, C, 9])
        conv_neg = sb("conv_neg", [C, C, 9])
        conv_sign = sb("conv_sign", [C, 9, 2, C])
        conv_st = sb("conv_st", [P, 4, 3, P], F32R)
        wq_st, wk_st = sb("wq_st", [P, 4, U]), sb("wk_st", [P, 4, U])
        wv_st = sb("wv_st", [P, U])
        wo_st, den_st = sb("wo_st", [P, C]), sb("den_st", [P, C])
        bo_col = sb("bo_col", [P, 1])
        xin = sb("xin", [P, S])
        xpk = sb("xpk", [P, HALF])
        pad = sb("pad", [P, HW + 2, PADW], F32R)
        stats, mv, mv2 = sb("stats", [P, MC, 6]), sb("mv", [P, 2]), sb("mv2", [P, 2])
        gm, gsq, gvar, gln, gs, gb = (sb(n, [P, 2]) for n in ("gm", "gsq", "gvar", "gln", "gs", "gb"))
        tres, xn = sb("tres", [P, HALF]), sb("xn", [P, HALF])
        sq, rstd = sb("sq", [P, 2, CW]), sb("rstd", [P, 2, CW])
        base = sb("base", [P, 2, HALF])
        qs = [sb(f"qs{j}", [P, SP], F32R) for j in range(2)]
        ks = [sb(f"ks{j}", [P, SP], F32R) for j in range(2)]
        vs = [sb(f"vs{j}", [P, KB, C]) for j in range(2)]
        part_max, block_max = sb("part_max", [P, KB, MC]), sb("block_max", [P, NMR * MR])
        neg_max = sb("neg_max", [P, KS + NMR * MR], F32R)
        probs = sb("probs", [P, 4, 2 * QW])
        osb = sb("osb", [P, 2, 2 * QW])
        rden, onorm = sb("rden", [P, QW]), sb("onorm", [P, QW])
        t2 = sb("t2", [P, 2, HALF])
        xn2 = sb("xn2", [P, HALF])
        sq2, rstd2 = sb("sq2", [P, 2, CW]), sb("rstd2", [P, 2, CW])
        hi, lo = sb("hi", [P, HALF], F32R), sb("lo", [P, HALF], F32R)

        pb = [ctx.enter_context(nc.psum_tensor(f"bank{j}", [P, 512], F32)) for j in range(8)]
        s_bank, o_bank, m_bank, x0, x1 = pb[0:3], pb[3], pb[4:6], pb[6], pb[7]

        conv_loaded, loaded_w, weights_ready, setup = sem("conv_loaded"), sem("loaded_w"), sem("weights_ready"), sem("setup")
        signs_ready, conv_turned, fills_done = sem("signs_ready"), sem("conv_turned"), sem("fills_done")
        x_loaded, xpk_loaded = sem("x_loaded"), sem("xpk_loaded")
        dve_chain, pool_chain, dve_passed, pool_passed = sem("dve_chain"), sem("pool_chain"), sem("dve_passed"), sem("pool_passed")
        moments_ready, pair_done, gvar_ready, gln_ready, gs_ready, gb_ready = (
            sem(n) for n in ("moments_ready", "pair_done", "gvar_ready", "gln_ready", "gs_ready", "gb_ready"))
        pad_hi, pad_lo = sem("pad_hi"), sem("pad_lo")
        conv_done, tres_ready, mean_done, cent_ready, sq_ready, var_done, rln_ready, rstd_ready, xn_ready, base_ready = (
            sem(n) for n in ("conv_done", "tres_ready", "mean_done", "cent_ready", "sq_ready", "var_done", "rln_ready", "rstd_ready", "xn_ready", "base_ready"))
        m_done, part_hi, m_used = sem("m_done"), sem("part_hi"), sem("m_used")
        v_done, v_ready = sem("v_done"), sem("v_ready")
        negmax_ready, row_done, row_ready = sem("negmax_ready"), sem("row_done"), sem("row_ready")
        s_done, p_ready, o_done, o_saved, proj_done, t2_ready = (sem(n) for n in ("s_done", "p_ready", "o_done", "o_saved", "proj_done", "t2_ready"))
        mean2_done, cent2_ready, sq2_ready, var2_done, rln2_ready, rstd2_ready, xn2_ready, feat_ready, hi_ready, lo_ready = (
            sem(n) for n in ("mean2_done", "cent2_ready", "sq2_ready", "var2_done", "rln2_ready", "rstd2_ready", "xn2_ready", "feat_ready", "hi_ready", "lo_ready"))
        t2_stored, hi_stored, lo_stored = sem("t2_stored"), sem("hi_stored"), sem("lo_stored")

        def proj_cols(tile, part, q, n):
            if n < 2:
                return tile[part, 0:S].rearrange("p (c a i) -> p c a i", a=2, i=QW)[:, q * CW // QW:(q + 1) * CW // QW, n, :]
            return tile[part, (n - 2) * HALF + q * CW:(n - 2) * HALF + (q + 1) * CW]

        def piece(tile, q):
            return tile[:, q * CW:(q + 1) * CW]

        with nc.Block() as block1:
            @block1.sync
            def _(sp):
                def load(dst, src):
                    sp.dma_start(dst, src).then_inc(loaded_w, 16)
                sp.dma_start(conv_raw[:], conv_w.rearrange("o i a b -> o i (a b)")).then_inc(conv_loaded, 16)
                load(ident[:], ident_in)
                load(block[:], block_in)
                load(pair[:], pair_in)
                for h in range(2):
                    rows = slice(h * C, (h + 1) * C)
                    for r in range(4):
                        load(wq_st[rows, r, :], w_q)
                        load(wk_st[rows, r, :], w_k)
                    load(wv_st[rows, :], w_v)
                    load(bo_col[rows, :], b_o.rearrange("(c a) -> c a", a=1))
                sp.wait_ge(fills_done, 1)
                load(wo_st[0:U, :], w_o)
                load(wo_st[C:C + U, :], w_o)

                def fetch(image):
                    n = image.number()
                    if image.c or image.t is not None:
                        sp.wait_ge(pad_hi, image.count(CH, 0))
                        sp.wait_ge(pad_lo, image.count(CH, 0))
                        sp.wait_ge(tres_ready, image.count(CH, 0))
                    src = x_flat[bass.ds(n, 1)].rearrange("i c n -> (i c) n")
                    for h in range(2):
                        sp.dma_start(xin[h * C:(h + 1) * C, :], src).then_inc(x_loaded, 16)
                    for h in range(2):
                        sp.dma_start(xpk[h * C:(h + 1) * C, :].rearrange("c (r w) -> c r w", w=HW),
                                     x_rows[bass.ds(n, 1), h].rearrange("i c r w -> (i c) r w")).then_inc(xpk_loaded, 16)

                def store(image):
                    n, par = image.number(), image.parity

                    def to(dram):
                        return dram[bass.ds(n, 1)].rearrange("i a c n -> (i a c) n")
                    sp.wait_ge(t2_ready, image.count(4 * QC, 4 * QC))
                    sp.dma_start(to(t2_dram), t2[:, par, :]).then_inc(t2_stored, 16)
                    sp.wait_ge(hi_ready, image.count(CH, CH))
                    sp.dma_start(to(hi_dram), hi[:].bitcast(F32)).then_inc(hi_stored, 16)
                    sp.wait_ge(lo_ready, image.count(CH, CH))
                    sp.dma_start(to(lo_dram), lo[:].bitcast(F32)).then_inc(lo_stored, 16)

                fetch(Image(0))
                fetch(Image(1))
                fetch(Image(2))
                store(Image(0))
                fetch(Image(3))
                store(Image(1))
                loops = (images - 4) // 2
                with sp.Fori(0, loops) as t:
                    for j in range(2):
                        fetch(Image(4 + j, t))
                        store(Image(2 + j, t))
                store(Image(images - 2))
                store(Image(images - 1))
                sp.wait_ge(t2_stored, 16 * images)
                sp.wait_ge(hi_stored, 16 * images)
                sp.wait_ge(lo_stored, 16 * images)

            @block1.gpsimd
            def _(gp):
                gp.memset(wo_st[:], 0.0).then_inc(fills_done, 1)
                gp.memset(den_st[:], 0.0)
                gp.memset(pad[:].bitcast(F32), 0.0)
                gp.memset(conv_st[:].bitcast(F32), 0.0)
                gp.memset(eps5[:], 1e-5)
                gp.memset(neg_max[:].bitcast(F32), 0.0)
                gp.memset(feat[:], 0.0)
                gp.memset(probs[:], 0.0)
                for j in range(2):
                    gp.memset(qs[j][:].bitcast(F32), 0.0)
                    gp.memset(ks[j][:].bitcast(F32), 0.0)
                    gp.memset(vs[j][:, :, 0:U], 0.0)
                    gp.memset(vs[j][:, :, U + 1:C], 0.0)
                    last = gp.memset(vs[j][:, :, U:U + 1], 1.0)
                last.then_inc(fills_done, 1)
                gp.wait_ge(fills_done, 3)

                def step(stage, kind, im, place, *a):
                    if kind == "pad":
                        r, = a
                        rows = slice(r * HW // CH, (r + 1) * HW // CH)
                        cols = slice(r * S // CH, (r + 1) * S // CH)
                        wait_apart(gp, pad_hi, im.count(CH, r + 1), pool_passed)
                        gp.tensor_scalar(xin[:, cols], xin[:, cols], gs[:, 0:1], gb[:, 0:1], ALU.mult, ALU.add).then_inc(pool_chain, 1)
                        gp.wait_ge(pool_chain, im.count(CH, 1 + r))
                        inner = pad[C:P, 1 + rows.start:1 + rows.stop, 1:1 + HW]
                        gp.tensor_tensor(inner, xin[C:P, cols].rearrange("c (h w) -> c h w", w=HW), inner.bitcast(F32), ALU.subtract).then_inc(pad_lo, 1)
                        gp.wait_ge(pad_lo, im.count(CH, r + 1))
                    elif (stage, kind) == ("prepare", "var"):
                        q, = a
                        gp.wait_ge(rstd_ready, im.count(CH, q + 1))
                        gp.tensor_tensor(piece(xn, q), piece(xn, q), rstd[:, q % 2, :], ALU.mult).then_inc(xn_ready, 1)
                        gp.wait_ge(xn_ready, im.count(CH, q + 1))
                        gp.tensor_tensor(piece(base[:, im.parity, :], q), piece(tres, q), piece(xn, q), ALU.add).then_inc(base_ready, 1)
                    elif (stage, kind) == ("norms", "var"):
                        q, = a
                        gp.wait_ge(rstd2_ready, im.count(CH, q + 1))
                        gp.tensor_tensor(piece(xn2, q), piece(xn2, q), rstd2[:, q % 2, :], ALU.mult).then_inc(xn2_ready, 1)
                        gp.wait_ge(xn2_ready, im.count(CH, q + 1))
                        gp.tensor_tensor(piece(feat, q), piece(feat, q), piece(xn2, q), ALU.add).then_inc(feat_ready, 1)
                        gp.wait_ge(hi_ready, im.count(CH, q + 1))
                        if q == 0:
                            wait(gp, lo_stored, im.count(16, 0))
                        gp.tensor_tensor(piece(lo, q), piece(xn2, q), piece(hi, q).bitcast(F32), ALU.subtract).then_inc(lo_ready, 1)

                walk(gp, images, ACT_LAG, step)

            @block1.vector
            def _(dve):
                v = nc.vector
                dve.wait_ge(fills_done, 2)
                v.memset(den_st[U:U + 1, :], 1.0)
                v.memset(den_st[C + U:C + U + 1, :], 1.0)
                for j in range(2):
                    v.memset(ks[j][KS:KS + 1, 0:S].bitcast(F32), 1.0)
                    last = v.memset(vs[j][C:P, KB - 1, :], 0.0)
                last.then_inc(fills_done, 1)
                dve.wait_ge(conv_loaded, 16)
                by_tap = conv_raw[:].rearrange("o i t -> o t i")
                v.tensor_scalar(conv_neg[:], conv_raw[:], 0.0, None, ALU.is_lt).then_inc(dve_chain, 1)
                v.tensor_scalar(conv_raw[:], conv_raw[:], 0.0, None, ALU.is_gt).then_inc(dve_chain, 1)
                dve.wait_ge(dve_chain, 2)
                for h in range(2):
                    last = v.tensor_tensor(conv_sign[:, :, h, :], by_tap, conv_neg[:].rearrange("o i t -> o t i"), ALU.subtract)
                last.then_inc(signs_ready, 1)
                dve.wait_ge(loaded_w, 16 * (3 + 2 * 10 + 2))
                v.tensor_copy(ident_r[:], ident[:]).then_inc(setup, 1)
                for tap in range(9):
                    dy, dx = tap // 3, tap % 3
                    dve.wait_ge(conv_turned, tap + 1)
                    v.tensor_copy(conv_st[:, dy, dx, 0:C], m_bank[tap % 2][:, 0:C])
                    v.tensor_copy(conv_st[:, dy + 1, dx, C:P], m_bank[tap % 2][:, 0:C]).then_inc(weights_ready, 1)

                def step(stage, kind, im, place, *a):
                    par = im.parity
                    if kind == "max":
                        b, m = a
                        dve.wait_ge(m_done, place.m(place.use + 1))
                        v.tensor_reduce(part_max[:, b, m:m + 1], m_bank[place.bank()][:, 0:MW], AX.X, ALU.max).then_inc(m_used, 1)
                    elif kind == "blockmax":
                        r, = a
                        blocks = slice(r * MR, min((r + 1) * MR, KB))
                        dve.wait_ge(m_used, place.m(place.after))
                        v.tensor_reduce(block_max[:, blocks], part_max[:, blocks, :], AX.X, ALU.max).then_inc(negmax_ready, 1)
                    elif kind == "negate":
                        r, = a
                        blocks = slice(r * MR, min((r + 1) * MR, KB))
                        dve.wait_ge(negmax_ready, im.count(2 * NMR, 2 * r + 1))
                        v.tensor_scalar(neg_max[:, KS + blocks.start:KS + blocks.stop], block_max[:, blocks], -1.0, None, ALU.mult).then_inc(negmax_ready, 1)
                    elif kind == "row":
                        r, = a
                        n0, n1 = r * MR * P, min((r + 1) * MR * P, S)
                        dve.wait_ge(m_done, place.m(place.use + 1))
                        v.tensor_copy(qs[par][KS:KS + 1, n0:n1], m_bank[place.bank()][KS:KS + 1, 0:n1 - n0]).then_inc(m_used, 1)
                    elif stage == "normalize":
                        if kind == "stats":
                            m, = a
                            if m == 0:
                                dve.wait_ge(x_loaded, im.count(32, 32))
                            v.bn_stats(stats[:, m, :], xin[:, m * MW:(m + 1) * MW]).then_inc(dve_chain, 1)
                        elif kind == "moments":
                            wait_apart(dve, dve_chain, im.count(MC + 4, 2 + MC), dve_passed)
                            v.bn_aggr(mv[:], stats[:]).then_inc(dve_chain, 1)
                            dve.wait_ge(dve_chain, im.count(MC + 4, 2 + MC + 1))
                            v.tensor_copy(mv2[:, 0:1], mv[:, 0:1])
                            v.scalar_tensor_tensor(mv2[:, 1:2], mv[:, 0:1], mv[:, 0:1], mv[:, 1:2], ALU.mult, ALU.add).then_inc(moments_ready, 1)
                        elif kind == "pair":
                            dve.wait_ge(pair_done, im.count(1, 1))
                            v.tensor_copy(gm[:], x0[:, 0:2]).then_inc(dve_chain, 1)
                            dve.wait_ge(dve_chain, im.count(MC + 4, 2 + MC + 2))
                            v.tensor_tensor(gsq[:, 0:1], gm[:, 0:1], gm[:, 0:1], ALU.mult).then_inc(dve_chain, 1)
                            dve.wait_ge(dve_chain, im.count(MC + 4, 2 + MC + 3))
                            v.tensor_tensor(gvar[:, 0:1], gm[:, 1:2], gsq[:, 0:1], ALU.subtract).then_inc(gvar_ready, 1)
                        elif kind == "shift":
                            dve.wait_ge(gs_ready, im.count(1, 1))
                            v.tensor_scalar(gsq[:, 1:2], gm[:, 0:1], -1.0, None, ALU.mult).then_inc(dve_chain, 1)
                            dve.wait_ge(dve_chain, im.count(MC + 4, 2 + MC + 4))
                            v.tensor_tensor(gb[:, 0:1], gsq[:, 1:2], gs[:, 0:1], ALU.mult).then_inc(gb_ready, 1)
                    elif stage == "prepare":
                        if kind == "conv":
                            q, = a
                            if q == 0:
                                dve.wait_ge(xpk_loaded, im.count(32, 32))
                            dve.wait_ge(conv_done, im.count(CH, q + 1))
                            v.tensor_tensor(piece(tres, q), x0[:, 0:CW], piece(xpk, q), ALU.add).then_inc(tres_ready, 1)
                        elif kind == "mean":
                            q, = a
                            dve.wait_ge(mean_done, im.count(CH, q + 1))
                            v.tensor_tensor(piece(xn, q), piece(tres, q), x0[:, 0:CW], ALU.subtract).then_inc(cent_ready, 1)
                        elif kind == "proj":
                            q, n = a
                            which = (qs, ks)[n // 2][par]
                            part = slice(U, 2 * U) if n < 2 else slice(2 * U, 3 * U)
                            dst, src = proj_cols(which, part, q, n), m_bank[place.bank()][part, 0:CW]
                            if n < 2:
                                src = src.rearrange("p (c i) -> p c i", i=QW)
                            dve.wait_ge(part_hi, im.count(4 * CH, 4 * q + n + 1))
                            v.tensor_tensor(dst, src, dst.bitcast(F32), ALU.subtract).then_inc(m_used, 1)
                    elif kind == "project":
                        c, = a
                        dve.wait_ge(proj_done, im.count(QC, c + 1))
                        if c == 0 and im.c:
                            wait(dve, t2_stored, im.count(16, -16))
                    elif kind == "divide":
                        c, n = a
                        cols = slice(c * QW, (c + 1) * QW)
                        if n < 2:
                            half = slice(n * QW // 2, (n + 1) * QW // 2)
                            v.reciprocal(rden[:, half], x1[:, QW + half.start:QW + half.stop]).then_inc(t2_ready, 1)
                            return
                        dve.wait_ge(t2_ready, im.count(4 * QC, 4 * c + n))
                        if n == 2:
                            v.tensor_tensor(onorm[:], x1[:, 0:QW], rden[:], ALU.mult).then_inc(t2_ready, 1)
                        else:
                            v.scalar_tensor_tensor(t2[:, par, cols], onorm[:], bo_col[:, 0:1], base[:, par, cols], ALU.add, ALU.add).then_inc(t2_ready, 1)
                    elif stage == "norms" and kind == "mean":
                        q, = a
                        if q == 0:
                            wait(dve, lo_ready, im.count(CH, 0))
                        dve.wait_ge(mean2_done, im.count(CH, q + 1))
                        v.tensor_tensor(piece(xn2, q), piece(t2[:, par, :], q), x1[:, 0:CW], ALU.subtract).then_inc(cent2_ready, 1)

                walk(dve, images, DVE_LAG, step)

            @block1.scalar
            def _(act):
                s = nc.scalar
                act.preload_act_table_set("natural_log_exp_and_others")
                act.wait_ge(fills_done, 3)

                def step(stage, kind, im, place, *a):
                    par = im.parity
                    if stage == "normalize":
                        if kind == "pair":
                            act.wait_ge(gvar_ready, im.count(1, 1))
                            s.activation(gln[:, 0:1], gvar[:, 0:1], ACT.Ln, bias=eps5[:]).then_inc(gln_ready, 1)
                            act.wait_ge(gln_ready, im.count(1, 1))
                            s.activation(gs[:, 0:1], gln[:, 0:1], ACT.Exp, scale=-0.5).then_inc(gs_ready, 1)
                        elif kind == "pad":
                            r, = a
                            if r == 0:
                                act.wait_ge(gb_ready, im.count(1, 1))
                                wait(act, conv_done, im.count(CH, 0))
                            rows = slice(1 + r * HW // CH, 1 + (r + 1) * HW // CH)
                            cols = slice(r * S // CH, (r + 1) * S // CH)
                            s.activation(pad[:, rows, 1:1 + HW], xin[:, cols].rearrange("c (h w) -> c h w", w=HW), ACT.Identity,
                                         bias=gb[:, 0:1], scale=gs[:, 0:1]).then_inc(pad_hi, 1)
                    elif stage == "prepare":
                        if kind == "mean":
                            q, = a
                            act.wait_ge(cent_ready, im.count(CH, q + 1))
                            s.activation(sq[:, q % 2, :], piece(xn, q), ACT.Square).then_inc(sq_ready, 1)
                        elif kind == "var":
                            q, = a
                            act.wait_ge(var_done, im.count(CH, q + 1))
                            s.activation(rstd[:, q % 2, :], x0[:, 0:CW], ACT.Ln, bias=eps5[:]).then_inc(rln_ready, 1)
                            act.wait_ge(rln_ready, im.count(CH, q + 1))
                            s.activation(rstd[:, q % 2, :], rstd[:, q % 2, :], ACT.Exp, scale=-0.5).then_inc(rstd_ready, 1)
                        elif kind == "proj":
                            q, n = a
                            src = m_bank[place.bank()][0:KS, 0:CW]
                            if n < 2:
                                src = src.rearrange("p (c i) -> p c i", i=QW)
                            act.wait_ge(m_done, place.m(place.use + 1))
                            s.activation(proj_cols((qs, ks)[n // 2][par], slice(0, KS), q, n), src, ACT.Copy).then_inc(part_hi, 1)
                        elif kind == "values":
                            n, = a
                            act.wait_ge(v_done, im.count(2, n + 1))
                            b0, b1 = (0, 13) if n == 0 else (13, KB - 1)
                            last = s.activation(vs[par][:, b0:b1, 0:U], x0[:, 0:(b1 - b0) * U].rearrange("p (b u) -> p b u", u=U), ACT.Copy)
                            if n == 1:
                                last = s.activation(vs[par][0:S - b1 * P, b1, 0:U], x0[0:S - b1 * P, (b1 - b0) * U:(b1 - b0 + 1) * U], ACT.Copy)
                            last.then_inc(v_ready, 1)
                    elif kind == "score":
                        c, k = a
                        n = c * KB + k
                        act.wait_ge(s_done, im.count(QC * KB, n + 1))
                        s.activation(probs[:, n % 4, :], s_bank[n % 3][:, 0:2 * QW], ACT.Exp, scale=SCALE).then_inc(p_ready, 1)
                    elif kind == "gather":
                        c, = a
                        act.wait_ge(o_done, im.count(QC, c + 1))
                        s.activation(osb[:, c % 2, :], o_bank[:, 0:2 * QW], ACT.Copy).then_inc(o_saved, 1)
                    elif stage == "norms" and kind != "divide":
                        q, = a
                        if kind == "mean":
                            act.wait_ge(cent2_ready, im.count(CH, q + 1))
                            s.activation(sq2[:, q % 2, :], piece(xn2, q), ACT.Square).then_inc(sq2_ready, 1)
                        elif kind == "var":
                            act.wait_ge(var2_done, im.count(CH, q + 1))
                            s.activation(rstd2[:, q % 2, :], x1[:, 0:CW], ACT.Ln, bias=eps5[:]).then_inc(rln2_ready, 1)
                            act.wait_ge(rln2_ready, im.count(CH, q + 1))
                            s.activation(rstd2[:, q % 2, :], rstd2[:, q % 2, :], ACT.Exp, scale=-0.5).then_inc(rstd2_ready, 1)
                        elif kind == "hi":
                            act.wait_ge(xn2_ready, im.count(CH, q + 1))
                            if q == 0:
                                wait(act, hi_stored, im.count(16, 0))
                            s.activation(piece(hi, q), piece(xn2, q), ACT.Copy).then_inc(hi_ready, 1)

                walk(act, images, ACT_LAG, step)

            @block1.tensor
            def _(pe):
                mm = nc.tensor.matmul
                pe.wait_ge(loaded_w, 16 * (3 + 2 * 10 + 2))
                pe.wait_ge(signs_ready, 1)
                for tap in range(9):
                    if tap >= 2:
                        pe.wait_ge(weights_ready, tap - 1)
                    mm(m_bank[tap % 2][:, 0:C], conv_sign[:, tap, :, :].rearrange("o h i -> o (h i)"), ident[0:C, 0:C], start=True, stop=True).then_inc(conv_turned, 1)
                pe.wait_ge(weights_ready, 9)
                pe.wait_ge(setup, 1)

                def step(stage, kind, im, place, *a):
                    par = im.parity
                    if kind == "max":
                        b, m = a
                        if (b, m) == (0, 0):
                            pe.wait_ge(m_used, place.m(place.use))
                        wait(pe, m_used, place.m(place.use - 1))
                        mm(m_bank[place.bank()][:, 0:MW], qs[par][0:KS, b * P:(b + 1) * P], ks[par][0:KS, m * MW:(m + 1) * MW], start=True, stop=True).then_inc(m_done, 1)
                    elif kind == "row":
                        r, = a
                        pe.wait_ge(negmax_ready, im.count(2 * NMR, 2 * r + 2))
                        wait(pe, m_used, place.m(place.use - 1))
                        for b in range(r * MR, min((r + 1) * MR, KB)):
                            last = mm(m_bank[place.bank()][0:KS + 1, b % MR * P:(b % MR + 1) * P], neg_max[:, b:b + KS + 1], ident_r[:], start=True, stop=True)
                        last.then_inc(m_done, 1)
                    elif kind == "score":
                        c, k = a
                        if k == 0:
                            wait(pe, m_used, place.m(place.after))
                        if k % 2 and k >= 3:
                            pe.wait_ge(p_ready, im.count(QC * KB, c * KB + k - 2))
                        mm(s_bank[(c * KB + k) % 3][:, 0:2 * QW], ks[par][0:KS + 1, k * P:(k + 1) * P], qs[par][0:KS + 1, c * 2 * QW:(c + 1) * 2 * QW],
                           start=True, stop=True).then_inc(s_done, 1)
                    elif kind == "value":
                        c, k = a
                        if k == 0:
                            wait(pe, o_saved, im.count(QC, c))
                        pe.wait_ge(p_ready, im.count(QC * KB, c * KB + min(k + 2, KB)))
                        for h in range(2):
                            half = slice(h * C, (h + 1) * C)
                            if k + 1 < KB:
                                mm(o_bank[half, 0:2 * QW], vs[par][:, k + h, :], probs[:, (c * KB + k + h) % 4, :], start=k == 0, stop=False)
                            else:
                                last = mm(o_bank[half, h * QW:(h + 1) * QW], vs[par][:, k, :], probs[:, (c * KB + k) % 4, h * QW:(h + 1) * QW], start=False, stop=True)
                        if k + 1 == KB:
                            last.then_inc(o_done, 1)
                    elif kind == "project":
                        c, = a
                        pe.wait_ge(o_saved, im.count(QC, c + 1))
                        if c == 0:
                            wait(pe, rln2_ready, im.count(CH, 0))
                        else:
                            pe.wait_ge(t2_ready, im.count(4 * QC, 4 * c - 1))
                        for n, weights in enumerate((wo_st, den_st)):
                            for h in range(2):
                                last = mm(x1[h * C:(h + 1) * C, n * QW:(n + 1) * QW], weights[:], osb[:, c % 2, h * QW:(h + 1) * QW], start=True, stop=True)
                        last.then_inc(proj_done, 1)
                    elif stage == "norms" and kind != "divide":
                        q, = a
                        if kind == "mean":
                            if q == 0:
                                pe.wait_ge(t2_ready, im.count(4 * QC, 4 * QC))
                            elif q == 1:
                                pe.wait_ge(cent2_ready, im.count(CH, 1))
                            else:
                                pe.wait_ge(rln2_ready, im.count(CH, q - 1))
                            mm(x1[:, 0:CW], block[:], piece(t2[:, par, :], q), start=True, stop=True).then_inc(mean2_done, 1)
                        elif kind == "var":
                            if q < 3:
                                pe.wait_ge(cent2_ready, im.count(CH, q + 2))
                            else:
                                pe.wait_ge(rln2_ready, im.count(CH, 3))
                            pe.wait_ge(sq2_ready, im.count(CH, q + 1))
                            mm(x1[:, 0:CW], block[:], sq2[:, q % 2, :], start=True, stop=True).then_inc(var2_done, 1)
                    elif kind == "pair":
                        pe.wait_ge(moments_ready, im.count(1, 1))
                        wait(pe, v_ready, im.count(2, 0))
                        mm(x0[:, 0:2], pair[:], mv2[:], start=True, stop=True).then_inc(pair_done, 1)
                    elif kind == "conv":
                        q, = a
                        pe.wait_ge(pad_lo, im.count(CH, min(q + 2, CH)))
                        if q == 0:
                            pe.wait_ge(gvar_ready, im.count(1, 1))
                        else:
                            pe.wait_ge(cent_ready, im.count(CH, q))
                        for r in range(4):
                            for dx in range(3):
                                top = 2 * CP * q + r
                                last = mm(x0[:, 0:CW].rearrange("p (r w) -> p r w", w=HW), conv_st[:, r, dx, :],
                                          pad[:, top:top + 2 * CP - 1:2, dx:dx + HW], start=r + dx == 0, stop=r + dx == 5)
                        last.then_inc(conv_done, 1)
                    elif kind == "mean":
                        q, = a
                        pe.wait_ge(tres_ready, im.count(CH, q + 1))
                        if q:
                            pe.wait_ge(rln_ready, im.count(CH, q))
                        mm(x0[:, 0:CW], block[:], piece(tres, q), start=True, stop=True).then_inc(mean_done, 1)
                    elif kind == "var":
                        q, = a
                        if q < 3:
                            pe.wait_ge(tres_ready, im.count(CH, q + 2))
                        else:
                            pe.wait_ge(cent_ready, im.count(CH, CH))
                        pe.wait_ge(sq_ready, im.count(CH, q + 1))
                        mm(x0[:, 0:CW], block[:], sq[:, q % 2, :], start=True, stop=True).then_inc(var_done, 1)
                    elif kind == "proj":
                        q, n = a
                        if n == 0:
                            pe.wait_ge(xn_ready, im.count(CH, q + 1))
                        wait(pe, m_used, place.m(place.use - 1))
                        h, weights = n % 2, (wq_st, wk_st)[n // 2]
                        rows = slice(h * C, (h + 1) * C)
                        mm(m_bank[place.bank()][:, 0:CW], weights[rows].rearrange("p r u -> p (r u)"), xn[rows, q * CW:(q + 1) * CW], start=True, stop=True).then_inc(m_done, 1)
                    elif kind == "values":
                        n, = a
                        if n == 0:
                            pe.wait_ge(xn_ready, im.count(CH, CH))
                            pe.wait_ge(rln_ready, im.count(CH, CH))
                        else:
                            pe.wait_ge(v_ready, im.count(2, 1))
                        b0, b1 = (0, 13) if n == 0 else (13, KB)
                        for b in range(b0, b1):
                            at, end = b * P, min((b + 1) * P, S)
                            while at < end:
                                h, row = at // HALF, at % P
                                stop = min(end, (h + 1) * HALF, at + (P if row == 0 else 64 if row == 64 else 32))
                                last = mm(x0[row:row + stop - at, (b - b0) * U:(b - b0 + 1) * U], xn[h * C:(h + 1) * C, at - h * HALF:stop - h * HALF],
                                          wv_st[h * C:(h + 1) * C, :], start=True, stop=True)
                                at = stop
                        last.then_inc(v_done, 1)

                walk(pe, images, 0.0, step)


def rows_of(w):
    return w.rearrange("(e a) h k -> a h e k", a=2)


def expert_phase(nc, images, w_r, b_r, w1, b1, g1, be1, m1, v1, w2, b2, g2, be2, m2, v2, w3, b3, select_in,
                 t2_dram, hi_dram, lo_dram, out, ident, feat):
    out_rows = out.rearrange("i c (r a) w -> i a c r w", a=2)
    groups = images // 4
    ctx = ExitStack()
    with ctx:
        def sb(name, shape, dt=F32):
            return ctx.enter_context(nc.sbuf_tensor(name, shape, dt))

        def sem(name):
            return ctx.enter_context(nc.semaphore(name))

        eps3 = sb("eps3", [P, 1])
        select = sb("select", [EXP, EP, P])
        w1f = sb("w1f", [P, EXP * HID])
        w1h, w1l = sb("w1h", [P, EXP * HID], F32R), sb("w1l", [P, EXP * HID], F32R)
        w2f = sb("w2f", [P, EP, P])
        w3f = sb("w3f", [P, EP, C])
        g2row, v2row, r2row, s2row = (sb(n, [P, EXP * HID]) for n in ("g2row", "v2row", "r2row", "s2row"))
        cols = {n: sb("col_" + n, [P, EP]) for n in ("b1", "g1", "be1", "m1", "v1", "b2", "g2", "be2", "m2", "v2")}
        tmp = {n: sb("tmp_" + n, [P, EP]) for n in ("l1", "r1", "s1", "d1", "p1", "c1", "l2", "r2", "s2", "d2", "p2", "c2", "n2")}
        c2_st = sb("c2_st", [P, EP, EXP])
        b3f, b3w = sb("b3f", [EXP, C]), sb("b3w", [EXP, 2, C])
        wr_sb, br_row = sb("wr_sb", [P, EXP]), sb("br_row", [P, EXP])
        NB = 2 * RB
        logits, shifted, powers, gates = (sb(n, [P, NB, EXP]) for n in ("logits", "shifted", "powers", "gates"))
        top, total, inverse = sb("top", [P, NB]), sb("total", [P, NB]), sb("inverse", [P, NB])
        gates_t = sb("gates_t", [EXP, 2 * RW])
        gate_w = sb("gate_w", [P, EP, CW])
        bias_w = sb("bias_w", [P, CW])
        xs = sb("xs", [P, 4, CW], F32R)
        res = sb("res", [P, 2, CW])
        h1, h2 = sb("h1", [P, 2, 2, CW]), sb("h2", [P, 2, 2, CW])
        fin = sb("fin", [P, 2, CW])
        pb = [ctx.enter_context(nc.psum_tensor(f"ebank{j}", [P, 2, 512], F32)) for j in range(4)]
        bank1, bank2, bank3, bank4 = pb
        b_bank = (bank2, bank4)

        loaded, filled, cols_ready, row_ready, chain, w_ready = (sem(n) for n in ("loaded2", "filled2", "cols_ready", "rows_ready2", "chain2", "w_ready2"))
        c2_ready, b3_done, logits_done, shift_ready, powers_ready, gates_ready, turned, turn_saved = (
            sem(n) for n in ("c2_ready", "b3_done", "logits_done", "shift_ready", "powers_ready", "gates_ready", "turned", "turn_saved"))
        half_done = sem("half_done")
        gate_done, gate_saved, gate_passed = sem("gate_done"), sem("gate_saved"), sem("gate_passed")
        xs_loaded, res_loaded = ([sem(f"{n}{p}") for p in range(2)] for n in ("xs_loaded", "res_loaded"))
        a_done, c_done, res_ready, fin_ready, stored = ([sem(f"{n}{p}") for p in range(2)] for n in ("a_done", "c_done", "res_ready", "fin_ready", "stored"))
        a_half, h1_ready, b_done, h2_ready = (
            sem(n) for n in ("a_half", "h1_ready", "b_done", "h2_ready"))

        TURN_BANKS = -(-NB // 4)
        with nc.Block() as block2:
            @block2.sync
            def _(sp):
                def load(dst, src):
                    sp.dma_start(dst, src).then_inc(loaded, 16)
                load(select[:], select_in)
                for h in range(2):
                    load(w1f[h * C:(h + 1) * C, :].rearrange("d (e h) -> d e h", h=HID), w1.rearrange("e d h -> d e h"))
                    load(wr_sb[h * C:(h + 1) * C, :], w_r)
                    load(w3f[h * C:(h + 1) * C, :, :], rows_of(w3)[h])
                    for name, src in (("b1", b1), ("g1", g1), ("be1", be1), ("m1", m1), ("v1", v1), ("b2", b2), ("g2", g2), ("be2", be2), ("m2", m2), ("v2", v2)):
                        sp.dma_start(cols[name][h * C:(h + 1) * C, :], src.rearrange("(e a) h -> a h e", a=2)[h], allow_slow_non_contiguous=True).then_inc(loaded, 16)
                load(b3f[:], b3)
                load(br_row[:], b_r.partition_broadcast(P))
                load(g2row[:], g2.rearrange("e k -> (e k)").partition_broadcast(P))
                load(v2row[:], v2.rearrange("e k -> (e k)").partition_broadcast(P))
                sp.wait_ge(filled, 1)
                for h in range(2):
                    load(w2f[h * C:(h + 1) * C, :, h * HID:(h + 1) * HID], rows_of(w2)[h])
            LOADS = 16 * (1 + 2 * 13 + 4 + 2)

            @block2.gpsimd
            def _(gp):
                gp.memset(w2f[:], 0.0).then_inc(filled, 1)
                gp.memset(c2_st[:], 0.0)
                gp.memset(eps3[:], 1e-3).then_inc(filled, 1)

            @block2.scalar
            def _(act):
                s = nc.scalar
                act.preload_act_table_set("natural_log_exp_and_others")
                act.wait_ge(loaded, LOADS)
                act.wait_ge(filled, 2)
                s.activation(tmp["l1"][:], cols["v1"][:], ACT.Ln, bias=eps3[:])
                s.activation(tmp["l2"][:], cols["v2"][:], ACT.Ln, bias=eps3[:])
                s.activation(r2row[:], v2row[:], ACT.Ln, bias=eps3[:]).then_inc(row_ready, 1)
                act.wait_ge(row_ready, 1)
                s.activation(tmp["r1"][:], tmp["l1"][:], ACT.Exp, scale=-0.5)
                s.activation(tmp["r2"][:], tmp["l2"][:], ACT.Exp, scale=-0.5)
                s.activation(s2row[:], r2row[:], ACT.Exp, scale=-0.5).then_inc(row_ready, 1)
                act.wait_ge(shift_ready, 1)
                s.activation(powers[:], shifted[:], ACT.Exp).then_inc(powers_ready, 1)

            @block2.vector
            def _(dve):
                v = nc.vector
                links = [0]

                def link(ins):
                    links[0] += 1
                    ins.then_inc(chain, 1)
                    dve.wait_ge(chain, links[0])

                dve.wait_ge(loaded, LOADS)
                dve.wait_ge(filled, 2)
                link(v.tensor_copy(w1h[:], w1f[:]))
                v.tensor_tensor(w1l[:], w1f[:], w1h[:].bitcast(F32), ALU.subtract)
                dve.wait_ge(row_ready, 2)
                for n in "12":
                    v.tensor_tensor(tmp["s" + n][:], cols["g" + n][:], tmp["r" + n][:], ALU.mult)
                    link(v.tensor_tensor(tmp["d" + n][:], cols["b" + n][:], cols["m" + n][:], ALU.subtract))
                    link(v.tensor_tensor(tmp["p" + n][:], tmp["d" + n][:], tmp["s" + n][:], ALU.mult))
                    link(v.tensor_tensor(tmp["c" + n][:], tmp["p" + n][:], cols["be" + n][:], ALU.add))
                v.tensor_scalar(tmp["n2"][:], tmp["c2"][:], -1.0, None, ALU.mult)
                link(v.tensor_tensor(s2row[:], s2row[:], g2row[:], ALU.mult))
                v.tensor_tensor(w2f[:], w2f[:], s2row[:].rearrange("p (e m) -> p e m", e=EP), ALU.mult)
                for e in range(EXP):
                    rows = slice((e % 2) * HID, (e % 2 + 1) * HID)
                    last = v.tensor_copy(c2_st[rows, e // 2, e:e + 1], tmp["c2"][rows, e // 2:e // 2 + 1])
                last.then_inc(c2_ready, 1)
                dve.wait_ge(b3_done, 1)
                v.tensor_tensor(b3w[:, 0, :], bank4[0:EXP, 0, 0:C], b3f[:], ALU.add)
                v.tensor_tensor(b3w[:, 1, :], bank4[0:EXP, 0, 0:C], b3f[:], ALU.add)
                dve.wait_ge(logits_done, 1)
                link(v.scalar_tensor_tensor(logits[:], bank4[:, 1, 0:NB * EXP].rearrange("p (b e) -> p b e", e=EXP), 1.0 / images,
                                            br_row[:].rearrange("p (b e) -> p b e", b=1).broadcast_to([P, NB, EXP]), ALU.mult, ALU.add))
                link(v.tensor_reduce(top[:], logits[:], AX.X, ALU.max))
                v.tensor_tensor(shifted[:], logits[:], top[:].rearrange("p (b e) -> p b e", e=1).broadcast_to([P, NB, EXP]), ALU.subtract).then_inc(shift_ready, 1)
                dve.wait_ge(powers_ready, 1)
                link(v.tensor_reduce(total[:], powers[:], AX.X, ALU.add))
                link(v.reciprocal(inverse[:], total[:]))
                v.tensor_tensor(gates[:], powers[:], inverse[:].rearrange("p (b e) -> p b e", e=1).broadcast_to([P, NB, EXP]), ALU.mult).then_inc(gates_ready, 1)
                for n in range(TURN_BANKS):
                    b1_, b0_ = min(4 * n + 4, NB), 4 * n
                    dve.wait_ge(turned, n + 1)
                    v.tensor_copy(gates_t[:, b0_ * P:b1_ * P], bank3[0:EXP, n % 2, 0:(b1_ - b0_) * P]).then_inc(turn_saved, 1)

            @block2.tensor
            def _(pe):
                mm = nc.tensor.matmul
                pe.wait_ge(c2_ready, 1)
                for e in range(EP):
                    last = mm(bank4[0:EXP, 0, 0:C], c2_st[:, e, :], w3f[:, e, :], start=e == 0, stop=e == EP - 1)
                last.then_inc(b3_done, 1)
                for b in range(NB):
                    if b == RB:
                        last.then_inc(half_done, 1)
                        pe.wait_ge(half_done, 1)
                    rows = slice(b // RB * C, (b // RB + 1) * C)
                    at = b % RB * P
                    last = mm(bank4[:, 1, b * EXP:(b + 1) * EXP], feat[rows, at:at + P], wr_sb[rows, :], start=True, stop=True)
                last.then_inc(logits_done, 1)
                pe.wait_ge(gates_ready, 1)
                for n in range(TURN_BANKS):
                    if n >= 2:
                        pe.wait_ge(turn_saved, n - 1)
                    for b in range(4 * n, min(4 * n + 4, NB)):
                        last = mm(bank3[0:EXP, n % 2, b % 4 * P:(b % 4 + 1) * P], gates[:, b, :], ident[:], start=True, stop=True)
                    last.then_inc(turned, 1)

        class Turn:

            def __init__(self, half, r, g=0):
                self.half, self.r, self.g = half, r, g

            def count(self, per, n):
                return self.half * (CH * groups * per) + self.r * (groups * per) + self.g * per + n

            def block_count(self, per, n):
                return self.half * (CH * per) + self.r * per + n

        def turns(engine, prologue, body, drain=None):
            with engine.Fori(0, 2) as half:
                with engine.Fori(0, CH) as r:
                    if prologue is not None:
                        prologue(Turn(half, r))
                    body(Turn(half, r, 0), False)
                    with engine.Fori(1, groups) as g:
                        body(Turn(half, r, g), True)
                    if drain is not None:
                        drain(Turn(half, r, groups))

        def part(dram, turn, j):
            return dram[bass.ds(turn.g * 4 + j, 1), bass.ds(turn.half, 1), :, bass.ds(turn.r * CW, CW)].rearrange("i a c n -> (i a c) n")

        with nc.Block() as block3:
            @block3.sync
            def _(sp):
                def body(turn, _):
                    for p in range(2):
                        sp.wait_ge(a_done[p], turn.count(1, 0))
                        for j in (2 * p, 2 * p + 1):
                            sp.dma_start(xs[0:C, j, :].bitcast(F32), part(hi_dram, turn, j)).then_inc(xs_loaded[p], 16)
                            sp.dma_start(xs[C:P, j, :].bitcast(F32), part(lo_dram, turn, j)).then_inc(xs_loaded[p], 16)
                    for p in range(2):
                        sp.wait_ge(fin_ready[p], turn.count(1, 0))
                        for h in range(2):
                            sp.dma_start(res[h * C:(h + 1) * C, p, :], part(t2_dram, turn, 2 * p + h)).then_inc(res_loaded[p], 16)
                turns(sp, None, body)

            @block3.gpsimd
            def _(gp):
                def body(turn, _):
                    for p in range(2):
                        gp.wait_ge(res_loaded[p], turn.count(32, 32))
                        if p == 0:
                            gp.wait_ge(gate_saved, turn.block_count(EP + 1, EP + 1))
                        gp.tensor_tensor(res[:, p, :], res[:, p, :], bias_w[:], ALU.add).then_inc(res_ready[p], 1)
                    for p in range(2):
                        gp.wait_ge(fin_ready[p], turn.count(1, 1))
                        for h in range(2):
                            dst = out_rows[bass.ds(turn.g * 4 + 2 * p + h, 1), bass.ds(turn.half, 1), :, bass.ds(turn.r * CP, CP), :]
                            gp.dma_start(dst.rearrange("i a c r w -> (i a c) r w"), fin[h * C:(h + 1) * C, p, :].rearrange("c (r w) -> c r w", w=HW)).then_inc(stored[p], 16)
                turns(gp, None, body)
                for p in range(2):
                    gp.wait_ge(stored[p], 16 * 2 * 2 * CH * groups)

            @block3.scalar
            def _(act):
                s = nc.scalar

                def prologue(turn):
                    act.wait_ge(fin_ready[1], turn.block_count(groups, 0))
                    act.wait_ge(res_ready[1], turn.block_count(groups, 0))
                    for e in range(EP + 1):
                        act.wait_ge(gate_done, turn.block_count(EP + 1, e + 1))
                        s.activation(gate_w[:, e, :] if e < EP else bias_w[:], bank4[:, e % 2, 0:CW], ACT.Copy).then_inc(gate_saved, 1)

                def body(turn, _):
                    for n in range(2 * EP):
                        act.wait_ge(a_half, turn.count(2 * EP, n + 1))
                        e = n % EP
                        s.activation(h1[:, n % 2, :, :], bank1[:, :, 0:CW], ACT.Relu, bias=tmp["c1"][:, e:e + 1], scale=tmp["s1"][:, e:e + 1]).then_inc(h1_ready, 1)
                turns(act, prologue, body)

            @block3.vector
            def _(dve):
                v = nc.vector

                def body(turn, carried):
                    for n in range(2 * EP):
                        e = n % EP
                        if n == 0:
                            dve.wait_ge(gate_saved, turn.block_count(EP + 1, EP))
                        dve.wait_ge(b_done, turn.count(2 * EP, n + 1))
                        v.scalar_tensor_tensor(h2[:, n % 2, :, :], b_bank[n % 2][:, :, 0:CW], tmp["n2"][:, e:e + 1],
                                               gate_w[:, e:e + 1, :].broadcast_to([P, 2, CW]), ALU.max, ALU.mult).then_inc(h2_ready, 1)
                        if n == 0 and carried:
                            finish(turn, -1)
                        if n == EP:
                            finish(turn, 0)

                def finish(turn, p):
                    now, p = turn.count(1, p + 1 if p == 0 else 0), p % 2
                    dve.wait_ge(c_done[p], now)
                    dve.wait_ge(res_ready[p], now)
                    dve.wait_ge(stored[p], now * 32 - 32)
                    v.tensor_tensor(fin[:, p, :], bank3[:, p, 0:CW], res[:, p, :], ALU.add).then_inc(fin_ready[p], 1)

                def drain(turn):
                    finish(turn, -1)
                turns(dve, None, body, drain)

            @block3.tensor
            def _(pe):
                mm = nc.tensor.matmul

                def prologue(turn):
                    for e in range(EP + 1):
                        wait_apart(pe, gate_saved, turn.block_count(EP + 1, max(e - 1, 0)), gate_passed)
                        weights = select[:, e, :] if e < EP else b3w[:].rearrange("e a c -> e (a c)")
                        mm(bank4[:, e % 2, 0:CW], weights, gates_t[:, bass.ds(turn.half * RW + turn.r * CW, CW)], start=True, stop=True).then_inc(gate_done, 1)

                def layer1(turn, n):
                    p, e = n // EP, n % EP
                    if e == 0:
                        pe.wait_ge(xs_loaded[p], turn.count(64, 64))
                    pe.wait_ge(h1_ready, turn.count(2 * EP, n))
                    for j in range(2):
                        mm(bank1[:, j, 0:CW], w1h[:, e * P:(e + 1) * P], xs[:, 2 * p + j, :], start=True, stop=False)
                        last = mm(bank1[:, j, 0:CW], w1l[:, e * P:(e + 1) * P], xs[:, 2 * p + j, :], start=False, stop=True)
                    last.then_inc(a_half, 1)

                def layer2(turn, n):
                    pe.wait_ge(h1_ready, turn.count(2 * EP, n + 1))
                    if n >= 0:
                        pe.wait_ge(h2_ready, turn.count(2 * EP, max(n - 1, 0)))
                    for j in range(2):
                        last = mm(b_bank[n % 2][:, j, 0:CW], w2f[:, n % EP, :], h1[:, n % 2, j, :], start=True, stop=True)
                        if j == 0 and n % EP == EP - 1:
                            last.then_inc(a_done[n // EP % 2], 1)
                    last.then_inc(b_done, 1)

                def layer3(turn, n):
                    p, e = n // EP % 2, n % EP
                    if e == 0:
                        pe.wait_ge(fin_ready[p], turn.count(1, 0))
                    pe.wait_ge(h2_ready, turn.count(2 * EP, n + 1))
                    for j in range(2):
                        last = mm(bank3[j * C:(j + 1) * C, p, 0:CW], w3f[:, e, :], h2[:, n % 2, j, :], start=e == 0, stop=e == EP - 1)
                    if e == EP - 1:
                        last.then_inc(c_done[p], 1)

                def body(turn, carried):
                    for n in range(2 * EP):
                        layer1(turn, n)
                        if n >= 1 or carried:
                            layer2(turn, n - 1)
                        if n >= 2 or carried:
                            layer3(turn, n - 2)

                def drain(turn):
                    layer2(turn, -1)
                    layer3(turn, -2)
                    layer3(turn, -1)
                turns(pe, prologue, body, drain)


def build(nc, images, x, conv_w, w_q, w_k, w_v, w_o, b_o, w_r, b_r, w1, b1, g1, be1, m1, v1,
          w2, b2, g2, be2, m2, v2, w3, b3, ident_in, block_in, pair_in, select_in, out):
    t2_dram = nc.dram_tensor("t2_dram", (images, 2, C, HALF), F32).ap()
    hi_dram = nc.dram_tensor("hi_dram", (images, 2, C, HALF), F32).ap()
    lo_dram = nc.dram_tensor("lo_dram", (images, 2, C, HALF), F32).ap()
    with nc.sbuf_tensor("ident", [P, P], F32) as ident, nc.sbuf_tensor("feat", [P, RW], F32) as feat:
        attention_phase(nc, images, x, conv_w, w_q, w_k, w_v, w_o, b_o, ident_in, block_in, pair_in, t2_dram, hi_dram, lo_dram, ident, feat)
        expert_phase(nc, images, w_r, b_r, w1, b1, g1, be1, m1, v1, w2, b2, g2, be2, m2, v2, w3, b3, select_in,
                     t2_dram, hi_dram, lo_dram, out, ident, feat)


INPUTS = ["x", "L0_conv_weight", "L1_attn_W_q", "L1_attn_W_k", "L1_attn_W_v", "L1_attn_W_o", "L1_attn_b_o", "L1_ffn_Wr", "L1_ffn_br",
          "L1_ffn_W1", "L1_ffn_b1", "L1_ffn_g1", "L1_ffn_be1", "L1_ffn_m1", "L1_ffn_v1",
          "L1_ffn_W2", "L1_ffn_b2", "L1_ffn_g2", "L1_ffn_be2", "L1_ffn_m2", "L1_ffn_v2", "L1_ffn_Wo", "L1_ffn_bo"]


def constants():
    n = np.arange(P)
    ident = np.eye(P, dtype=np.float32)
    block = (n[:, None] // C == n[None, :] // C).astype(np.float32) / C
    pair = (n[:, None] // 2 == n[None, :] // 2).astype(np.float32) / 2
    expert = 2 * np.arange(EP)[:, None] + n[None, :] // HID
    select = (np.arange(EXP)[:, None, None] == expert[None]).astype(np.float32)
    return {"ident": ident, "block": block, "pair": pair, "select": select}


def kernel(**inputs):
    import concourse.bacc as bacc
    from concourse.bass_utils import run_bass_kernel_spmd

    nc = bacc.Bacc("TRN2", target_bir_lowering=False, num_devices=1)
    arrays, args = {}, []
    for name, a in [(n, inputs[n]) for n in INPUTS] + list(constants().items()):
        a = np.ascontiguousarray(a)
        arrays[f"in_{name}_dram"] = a
        args.append(nc.dram_tensor(f"in_{name}_dram", a.shape, F32, kind="ExternalInput").ap())
    shape = tuple(inputs["x"].shape)
    out = nc.dram_tensor("out_dram", shape, F32, kind="ExternalOutput").ap()
    build(nc, shape[0], *args, out)
    result = run_bass_kernel_spmd(nc, [arrays], core_ids=[0])
    return result.results[0]["out_dram"]
```
